# Optimizing a Trainium2 kernel written in Bass

```python
import numpy as np
import jax
import jax.numpy as jnp

def _softmax(x, axis=-1):
    return jax.nn.softmax(x, axis=axis)

def _gelu(x):
    return jax.nn.gelu(x, approximate=True)

def _silu(x):
    return jax.nn.silu(x)

def _sigmoid(x):
    return jax.nn.sigmoid(x)

def _layernorm(x, axis=-1, eps=1e-05):
    m = jnp.mean(x, axis=axis, keepdims=True)
    v = jnp.var(x, axis=axis, keepdims=True)
    return (x - m) / jnp.sqrt(v + eps)

def _scatter_add(tgt, idx, src, axis=0):
    return tgt.at[idx].add(src)

def _segment_sum(src, seg, n):
    return jax.ops.segment_sum(src, seg, n)
kernel_name = 'mk_hybrid_d1_jaxref_r8_0c09b9'

def setup_inputs(seed: int=0):
    np.random.seed(seed)
    _w = jnp.asarray

    def _L0_attn_a_setup():
        import jax, jax.numpy as jnp
        import numpy as np
        B, T, C = (2, 256, 128)
        N_HEAD = 16
        WINDOW = 64
        ROPE_BASE = 10000.0

        def _apply_rotary(x, cos, sin):
            d = x.shape[-1] // 2
            x1, x2 = (x[..., :d], x[..., d:])
            return jnp.concatenate([x1 * cos + x2 * sin, -x1 * sin + x2 * cos], axis=-1)
        key = jax.random.key(seed)
        k1, k2, k3 = jax.random.split(key, 3)
        x = jax.random.normal(k1, (B, T, C), dtype=jnp.float32)
        w_attn = jax.random.normal(k2, (3 * C, C), dtype=jnp.float32) * 0.02
        w_proj = jax.random.normal(k3, (C, C), dtype=jnp.float32) * 0.02
        return {'x': x, 'w_attn': w_attn, 'w_proj': w_proj}
    _L0_attn_a_in = _L0_attn_a_setup()

    def _L0_attn_b_setup():
        import jax, jax.numpy as jnp
        import numpy as np
        D_MODEL, D_STATE, DT_RANK = (128, 16, 64)
        DT_MIN, DT_MAX = (0.001, 0.1)
        key = jax.random.key(seed)
        ks = jax.random.split(key, 8)
        B, L = (4, 256)
        x = jax.random.normal(ks[0], (B, L, D_MODEL), jnp.float32)
        A_log = jnp.log(jnp.tile(jnp.arange(1, D_STATE + 1, dtype=jnp.float32), (D_MODEL, 1)))
        D = jnp.ones((D_MODEL,), jnp.float32)
        dt_std = DT_RANK ** (-0.5)
        dt_proj_w = jax.random.uniform(ks[1], (D_MODEL, DT_RANK), jnp.float32, -dt_std, dt_std)
        dt = jnp.exp(jax.random.uniform(ks[2], (D_MODEL,), jnp.float32) * (np.log(DT_MAX) - np.log(DT_MIN)) + np.log(DT_MIN))
        dt_proj_b = dt + jnp.log(-jnp.expm1(-dt))
        scale = D_MODEL ** (-0.5)
        x_proj_w = jax.random.normal(ks[3], (DT_RANK, D_MODEL), jnp.float32) * scale
        B_proj_w = jax.random.normal(ks[4], (D_STATE, D_MODEL), jnp.float32) * scale
        C_proj_w = jax.random.normal(ks[5], (D_STATE, D_MODEL), jnp.float32) * scale
        return dict(x=x, A_log=A_log, D=D, dt_proj_w=dt_proj_w, dt_proj_b=dt_proj_b, x_proj_w=x_proj_w, B_proj_w=B_proj_w, C_proj_w=C_proj_w)
    _L0_attn_b_in = _L0_attn_b_setup()

    def _L0_ffn_setup():
        import jax, jax.numpy as jnp
        import numpy as np
        E = 8
        TOP_K = 2
        D = 128
        H = 2 * D
        key = jax.random.key(seed)
        k0, k1, k2, k3, k4 = jax.random.split(key, 5)
        scale = 0.02
        x = jax.random.normal(k0, (4, 256, D), dtype=jnp.float32)
        Wg = jax.random.normal(k1, (D, E), dtype=jnp.float32) * scale
        W1 = jax.random.normal(k2, (E, D, H), dtype=jnp.float32) * scale
        W2 = jax.random.normal(k3, (E, D, H), dtype=jnp.float32) * scale
        W3 = jax.random.normal(k4, (E, H, D), dtype=jnp.float32) * scale
        return {'x': x, 'Wg': Wg, 'W1': W1, 'W2': W2, 'W3': W3}
    _L0_ffn_in = _L0_ffn_setup()
    _d = {'L0_attn_a_x': _L0_attn_a_in['x'], 'L0_attn_a_w_attn': _L0_attn_a_in['w_attn'], 'L0_attn_a_w_proj': _L0_attn_a_in['w_proj'], 'L0_attn_b_A_log': _L0_attn_b_in['A_log'], 'L0_attn_b_D': _L0_attn_b_in['D'], 'L0_attn_b_dt_proj_w': _L0_attn_b_in['dt_proj_w'], 'L0_attn_b_dt_proj_b': _L0_attn_b_in['dt_proj_b'], 'L0_attn_b_x_proj_w': _L0_attn_b_in['x_proj_w'], 'L0_attn_b_B_proj_w': _L0_attn_b_in['B_proj_w'], 'L0_attn_b_C_proj_w': _L0_attn_b_in['C_proj_w'], 'L0_ffn_Wg': _L0_ffn_in['Wg'], 'L0_ffn_W1': _L0_ffn_in['W1'], 'L0_ffn_W2': _L0_ffn_in['W2'], 'L0_ffn_W3': _L0_ffn_in['W3']}
    _x0 = _d['L0_attn_a_x']
    _d['L0_attn_a_x'] = jax.random.normal(jax.random.fold_in(jax.random.key(seed), 1), (8, 512, 128), dtype=_x0.dtype)
    del _x0
    return _d

def reference(L0_attn_a_x, L0_attn_a_w_attn, L0_attn_a_w_proj, L0_attn_b_A_log, L0_attn_b_D, L0_attn_b_dt_proj_w, L0_attn_b_dt_proj_b, L0_attn_b_x_proj_w, L0_attn_b_B_proj_w, L0_attn_b_C_proj_w, L0_ffn_Wg, L0_ffn_W1, L0_ffn_W2, L0_ffn_W3):

    def _L0_attn_a_ref(x, w_attn, w_proj):
        import jax, jax.numpy as jnp
        import numpy as np
        B, T, C = (2, 256, 128)
        N_HEAD = 16
        WINDOW = 64
        ROPE_BASE = 10000.0

        def _apply_rotary(x, cos, sin):
            d = x.shape[-1] // 2
            x1, x2 = (x[..., :d], x[..., d:])
            return jnp.concatenate([x1 * cos + x2 * sin, -x1 * sin + x2 * cos], axis=-1)
        Bb, Tt, Cc = x.shape
        H = N_HEAD
        D = Cc // H
        qkv = x @ w_attn.T
        q, k, v = jnp.split(qkv, 3, axis=2)
        q = q.reshape(Bb, Tt, H, D)
        k = k.reshape(Bb, Tt, H, D)
        v = v.reshape(Bb, Tt, H, D)
        inv_freq = 1.0 / ROPE_BASE ** (jnp.arange(0, D, 2, dtype=jnp.float32) / D)
        freqs = jnp.outer(jnp.arange(Tt, dtype=jnp.float32), inv_freq)
        cos = jnp.cos(freqs)[None, :, None, :]
        sin = jnp.sin(freqs)[None, :, None, :]
        q = _apply_rotary(q, cos, sin)
        k = _apply_rotary(k, cos, sin)
        pos = jnp.arange(Tt)
        diff = pos[:, None] - pos[None, :]
        mask = (diff >= 0) & (diff <= WINDOW)
        scale = 1.0 / jnp.sqrt(jnp.asarray(D, dtype=q.dtype))
        scores = jnp.einsum('bqhd,bkhd->bhqk', q, k) * scale
        scores = jnp.where(mask[None, None, :, :], scores, jnp.asarray(-1e+30, scores.dtype))
        attn = jax.nn.softmax(scores, axis=-1)
        y = jnp.einsum('bhqk,bkhd->bqhd', attn, v).reshape(Bb, Tt, Cc)
        return y @ w_proj.T

    def _L0_attn_b_ref(x, A_log, D, dt_proj_w, dt_proj_b, x_proj_w, B_proj_w, C_proj_w):
        import jax, jax.numpy as jnp
        import numpy as np
        D_MODEL, D_STATE, DT_RANK = (128, 16, 64)
        DT_MIN, DT_MAX = (0.001, 0.1)
        A = -jnp.exp(A_log)
        r = jnp.einsum('blm,rm->blr', x, x_proj_w)
        delta = jax.nn.softplus(jnp.einsum('blr,dr->bld', r, dt_proj_w) + dt_proj_b)
        delta = jnp.clip(delta, DT_MIN, DT_MAX)
        Bm = jnp.einsum('blm,nm->bln', x, B_proj_w)
        Cm = jnp.einsum('blm,nm->bln', x, C_proj_w)

        def step(h, inp):
            x_t, d_t, B_t, C_t = inp
            A_bar = jnp.exp(d_t[:, :, None] * A)
            h = A_bar * h + (d_t * x_t)[:, :, None] * B_t[:, None, :]
            y_t = jnp.einsum('bdn,bn->bd', h, C_t)
            return (h, y_t)
        bsz = x.shape[0]
        h0 = jnp.zeros((bsz, D_MODEL, D_STATE), x.dtype)
        xs = (jnp.swapaxes(x, 0, 1), jnp.swapaxes(delta, 0, 1), jnp.swapaxes(Bm, 0, 1), jnp.swapaxes(Cm, 0, 1))
        _, ys = jax.lax.scan(step, h0, xs)
        y = jnp.swapaxes(ys, 0, 1) + D * x
        return y

    def _L0_ffn_ref(x, Wg, W1, W2, W3):
        import jax, jax.numpy as jnp
        import numpy as np
        E = 8
        TOP_K = 2
        D = 128
        H = 2 * D
        logits = jnp.einsum('bsd,de->bse', x, Wg)
        top_vals, top_idx = jax.lax.top_k(logits, TOP_K)
        probs = jax.nn.softmax(top_vals, axis=-1)
        onehot = jax.nn.one_hot(top_idx, E, dtype=x.dtype)
        weights = jnp.einsum('bsk,bske->bse', probs, onehot)
        out = jnp.zeros_like(x)
        for e in range(E):
            u = jnp.einsum('bsd,dh->bsh', x, W1[e])
            v = jnp.einsum('bsd,dh->bsh', x, W2[e])
            h = u * jax.nn.sigmoid(u) * v
            y = jnp.einsum('bsh,hd->bsd', h, W3[e])
            out = out + y * weights[..., e][..., None]
        return out
    x = L0_attn_a_x
    x = x + _L0_attn_a_ref(_layernorm(x, axis=-1), L0_attn_a_w_attn, L0_attn_a_w_proj)
    x = x + _L0_ffn_ref(_layernorm(x, axis=-1), L0_ffn_Wg, L0_ffn_W1, L0_ffn_W2, L0_ffn_W3)
    x = x + _L0_attn_b_ref(_layernorm(x, axis=-1), L0_attn_b_A_log, L0_attn_b_D, L0_attn_b_dt_proj_w, L0_attn_b_dt_proj_b, L0_attn_b_x_proj_w, L0_attn_b_B_proj_w, L0_attn_b_C_proj_w)
    x = x + _L0_ffn_ref(_layernorm(x, axis=-1), L0_ffn_Wg, L0_ffn_W1, L0_ffn_W2, L0_ffn_W3)
    return x

_drawn_inputs = setup_inputs


def setup_inputs(seed=0):
    import zlib

    import numpy as np

    out = dict(_drawn_inputs(seed))
    spreads = {'L0_attn_b_D': (1.0, 0.2)}
    factors = {'L0_attn_a_w_attn': 7.384,
     'L0_attn_a_w_proj': 7.201,
     'L0_ffn_Wg': 7.506,
     'L0_ffn_W1': 6.565,
     'L0_ffn_W2': 6.541,
     'L0_ffn_W3': 6.543}
    for name, (base, spread) in spreads.items():
        noise = np.random.default_rng([zlib.crc32(name.encode()), seed]).standard_normal(out[name].shape)
        drawn = base * np.exp(spread * noise) if base else spread * noise
        out[name] = jnp.asarray(drawn.astype(out[name].dtype))
    for name, factor in factors.items():
        out[name] = (out[name] * factor).astype(out[name].dtype)
    return out
```

```python
from contextlib import ExitStack

import numpy as np

import concourse.bass as bass
from concourse import mybir

ALU = mybir.AluOpType
ACT = mybir.ActivationFunctionType
AX_X = mybir.AxisListType.X
F32 = mybir.dt.float32
F16 = mybir.dt.float16
BF16 = mybir.dt.bfloat16
U32 = mybir.dt.uint32
I32 = mybir.dt.int32

P = 128
BATCH, T, C = 8, 512, 128
TILES = T // P
NT = BATCH * TILES
H, D = 16, 8
WINDOW = 64
QB = WINDOW
HG = 4
ROWS = 32
E, HID = 8, 256
HC = HID // P
NS = 16
DG = P // NS
G = C // DG
RANK = 64
EPS = 1e-5
DT_MIN, DT_MAX = 0.001, 0.1
UP = 1024.0
E_MAX = 0.1052
LOG_POLY = np.polynomial.chebyshev.Chebyshev.interpolate(
    lambda e: np.log1p(e) / e, 5, domain=[1e-9, E_MAX]).convert(kind=np.polynomial.Polynomial).coef


RSQRT_LINKS = 12


def rsqrt(dve, chained, v, y, t, first):
    chained(dve.tensor_scalar(v, v, EPS, None, ALU.add), first + 1)
    chained(dve.tensor_scalar(t.bitcast(I32), v.bitcast(I32), 1, None, ALU.logical_shift_right), first + 2)
    dve.tensor_scalar(y.bitcast(I32), t.bitcast(I32), -1.0, float(0x5F3759DF), ALU.mult, ALU.add)
    chained(dve.tensor_scalar(v, v, -0.5, None, ALU.mult), first + 3)
    for k in range(3):
        chained(dve.tensor_tensor(t, y, y, ALU.mult), first + 4 + 3 * k)
        chained(dve.tensor_tensor(t, t, v, ALU.mult), first + 5 + 3 * k)
        chained(dve.scalar_tensor_tensor(y, t, 1.5, y, ALU.add, ALU.mult), first + 6 + 3 * k)


def attention(nc, sb, psum, sem, X, K, W):
    PAD = QB
    st = sb("a_st", [P, NT, 6], F32)
    mv = sb("a_mv", [P, NT + 1, 2], F32)
    rstd = sb("a_rstd", [P, NT + 1, 1], F32)
    tmp = sb("a_tmp", [P, NT + 1], F32)
    xn = sb("a_xn", [P, C], F32)
    xnT = sb("a_xnT", [P, PAD + T], F32)
    rot_cos = sb("a_rot_cos", [P, 2 * C], F32)
    rot_sin = sb("a_rot_sin", [P, 2 * C], F32)
    rot = sb("a_rot", [P, 2 * C], F32)
    qs = sb("a_qs", [P, 2, H * ROWS], F16)
    ks = sb("a_ks", [P, 2, H * ROWS], F16)
    qkT = sb("a_qkT", [P, 2 * HG, PAD + T], F16)
    q2T = sb("a_q2T", [P, HG, P], F16)
    v_sb = sb("a_v", [P, 2 * TILES, H, D + 1], F32)
    mx = sb("a_mx", [P, H], F32)
    prob = sb("a_prob", [P, HG, HG * P], F32)
    rden = sb("a_rden", [P, H], F32)
    yn = sb("a_yn", [P, C], F32)
    yT = sb("a_yT", [P, C], F32)

    psS = [psum(f"a_psS{r}", [P, 512], F32) for r in range(HG)]
    psA = psum("a_psA", [P, 512], F32)
    psD = psum("a_psD", [P, 2 * HG, P], F16)
    psT = psum("a_psT", [P, 512], F32)
    psY = psum("a_psY", [P, 512], F32)

    start = sem("a_start")
    xn_ready = sem("a_xn_ready")
    xT_up = sem("a_xT_up")
    xT_ready = sem("a_xT_ready")
    qkv_up = sem("a_qkv_up")
    v_ready = sem("a_v_ready")
    rope_ready = sem("a_rope_ready")
    rot_ready = sem("a_rot_ready")
    hi_ready = sem("a_hi_ready")
    lo_ready = sem("a_lo_ready")
    st_up = sem("a_st_up")
    qkT_ready = sem("a_qkT_ready")
    s1_up = sem("a_s1_up")
    s1_used = sem("a_s1_used")
    m_ready = sem("a_m_ready")
    q2_up = sem("a_q2_up")
    q2_ready = sem("a_q2_ready")
    s2_up = sem("a_s2_up")
    p_ready = sem("a_p_ready")
    pv_up = sem("a_pv_up")
    yn_ready = sem("a_yn_ready")
    yT_up = sem("a_yT_up")
    yT_ready = sem("a_yT_ready")
    out_up = sem("a_out_up")
    x_done = sem("a_x_done")
    dve_step = sem("a_dve_step")
    STATS = 2 + RSQRT_LINKS
    DVE_STEPS = 2

    with nc.Block() as block:

        @block.gpsimd
        def _(pool):
            pool.memset(xnT[:, 0:PAD], 0.0).then_inc(start, 1)
            pool.memset(qkT[:, :, 0:PAD], 0.0).then_inc(start, 1)
            pool.memset(v_sb[:, :, :, D:D + 1], 1.0).then_inc(start, 1)
            pool.memset(qs[:], 0.0).then_inc(start, 1)
            pool.memset(ks[:], 0.0).then_inc(start, 1)
            pool.wait_ge(start, 5)
            for s in range(2):
                pool.memset(ks[:, s, :].rearrange("p (h r) -> p h r", r=ROWS)[:, :, 24:25], 1.0).then_inc(start, 1)

            def stack(t, s):
                q_out = qs[:, s, :].rearrange("p (h r) -> p h r", r=ROWS)
                k_out = ks[:, s, :].rearrange("p (h r) -> p h r", r=ROWS)
                q_in = rot[:, 0:C].rearrange("p (h d) -> p h d", d=D)
                k_in = rot[:, C:2 * C].rearrange("p (h d) -> p h d", d=D)
                pool.wait_ge(rope_ready, (t + 1) * 3)
                if s is not None:
                    pool.wait_ge(hi_ready, t * 2)
                pool.tensor_tensor(rot[:], rot_cos[:], rot_sin[:], ALU.add).then_inc(rot_ready, 1)
                pool.wait_ge(hi_ready, (t + 1) * 2)
                pool.wait_ge(rot_ready, t + 1)
                pool.tensor_tensor(q_out[:, :, 8:16], q_in, q_out[:, :, 0:8], ALU.subtract).then_inc(lo_ready, 1)
                pool.tensor_tensor(k_out[:, :, 16:24], k_in, k_out[:, :, 0:8], ALU.subtract).then_inc(lo_ready, 1)

            stack(0, 0)
            with pool.Fori(0, BATCH) as b:
                for i in range(TILES):
                    stack(b * TILES + (i + 1), (i + 1) % 2)

        @block.scalar
        def _(act):
            act.wait_ge(start, 7)

            def front(t, i):
                act.wait_ge(xT_up, t + 1)
                act.copy(xnT[:, PAD + i * P:PAD + (i + 1) * P], psT[:, 0:P]).then_inc(xT_ready, 1)
                act.wait_ge(rope_ready, (t + 1) * 3)
                act.copy(v_sb[:, 2 * i:2 * i + 2, :, 0:D],
                         psA[:, 256:512].rearrange("p (w h d) -> p w h d", w=2, d=D)).then_inc(v_ready, 1)
                s = i % 2
                q_out = qs[:, s, :].rearrange("p (h r) -> p h r", r=ROWS)
                k_out = ks[:, s, :].rearrange("p (h r) -> p h r", r=ROWS)
                q_in = rot[:, 0:C].rearrange("p (h d) -> p h d", d=D).unsqueeze(2).broadcast_to([P, H, 2, D])
                k_in = rot[:, C:2 * C].rearrange("p (h d) -> p h d", d=D).unsqueeze(2).broadcast_to([P, H, 2, D])
                act.wait_ge(rot_ready, t + 1)
                act.copy(q_out[:, :, 0:32].rearrange("p h (a d) -> p h a d", a=2)[:, :, :, 0:D], q_in).then_inc(hi_ready, 1)
                act.copy(k_out[:, :, 0:16].rearrange("p h (a d) -> p h a d", a=2), k_in).then_inc(hi_ready, 1)

            def stacks(t, i):
                act.wait_ge(st_up, t + 1)
                act.copy(qkT[:, :, PAD + i * P:PAD + (i + 1) * P], psD[:]).then_inc(qkT_ready, 1)

            def probs(t):
                act.wait_ge(q2_up, t + 1)
                act.copy(q2T[:], psD[:, 0:HG, :]).then_inc(q2_ready, 1)
                act.wait_ge(pv_up, t)
                for r in range(HG):
                    act.wait_ge(s2_up, t * HG + (r + 1))
                    act.activation(prob[:, r, :], psS[r][:], ACT.Exp, scale=float(D) ** -0.5).then_inc(p_ready, 1)

            def out(t):
                act.wait_ge(yT_up, t + 1)
                act.copy(yT[:], psT[:, 0:P]).then_inc(yT_ready, 1)

            front(0, 0)
            stacks(0, 0)
            with act.Fori(0, BATCH) as b:
                for i in range(TILES):
                    t = b * TILES + i
                    front(b * TILES + (i + 1), (i + 1) % TILES)
                    probs(t)
                    stacks(b * TILES + (i + 1), (i + 1) % TILES)
                    out(t)

        @block.vector
        def _(dve):
            dve.wait_ge(start, 7)

            def chained(ins, value):
                ins.then_inc(dve_step, 1)
                dve.wait_ge(dve_step, value)

            for t in range(NT):
                ins = dve.bn_stats(st[:, t, :], X[:, t, :])
            chained(ins, 1)
            dve.memset(mv[:, NT, :], 1.0)
            for t in range(NT):
                ins = dve.bn_aggr(mv[:, t, :], st[:, t, :])
            chained(ins, 2)
            rsqrt(dve, chained, mv[:, :, 1], rstd[:, :, 0], tmp[:], 2)

            def norm(t):
                dve.wait_ge(xT_up, t)
                dve.tensor_scalar(xn[:], X[:, t, :], mv[:, t, 0:1], rstd[:, t, :], ALU.subtract, ALU.mult).then_inc(xn_ready, 1)

            def rope(t, i):
                qk = psA[:, 0:256].rearrange("p (h a d) -> p h a d", a=2, d=4)
                o_cos = rot_cos[:].rearrange("p (h a d) -> p h a d", a=2, d=4)
                o_sin = rot_sin[:].rearrange("p (h a d) -> p h a d", a=2, d=4)
                cos = K["cos"][:, i, :].unsqueeze(1).broadcast_to([P, 4 * H, 4])
                sin = K["sin"][:, i, :].unsqueeze(1).broadcast_to([P, 2 * H, 4])
                nsin = K["nsin"][:, i, :].unsqueeze(1).broadcast_to([P, 2 * H, 4])
                dve.wait_ge(qkv_up, t + 1)
                dve.wait_ge(rot_ready, t)
                dve.tensor_tensor(rot_cos[:].rearrange("p (h d) -> p h d", d=4),
                                  psA[:, 0:256].rearrange("p (h d) -> p h d", d=4), cos, ALU.mult).then_inc(rope_ready, 1)
                dve.tensor_tensor(o_sin[:, :, 0, :], qk[:, :, 1, :], sin, ALU.mult).then_inc(rope_ready, 1)
                dve.tensor_tensor(o_sin[:, :, 1, :], qk[:, :, 0, :], nsin, ALU.mult).then_inc(rope_ready, 1)

            def maxima(t, s):
                for r in range(HG):
                    dve.wait_ge(s1_up, t * HG + (r + 1))
                    m = dve.tensor_reduce(mx[:].rearrange("p (g r) -> p g r", r=HG)[:, :, r],
                                          psS[r][:].rearrange("p (g k) -> p g k", g=HG), AX_X, ALU.max)
                    m.then_inc(s1_used, 1)
                dve.wait_ge(s1_used, (t + 1) * HG)
                q_out = qs[:, s, :].rearrange("p (h r) -> p h r", r=ROWS)
                dve.tensor_scalar(q_out[:, :, 24], mx[:], -1.0, None, ALU.mult).then_inc(m_ready, 1)

            def out(t):
                y = psY[:, 0:H * (D + 1)].rearrange("p (h d) -> p h d", d=D + 1)
                dve.wait_ge(pv_up, t + 1)
                chained(dve.reciprocal(rden[:], y[:, :, D]), STATS + t * DVE_STEPS + 1)
                dve.wait_ge(yT_up, t)
                dve.tensor_tensor(yn[:].rearrange("p (h d) -> p h d", d=D), y[:, :, 0:D],
                                  rden[:].unsqueeze(2).broadcast_to([P, H, D]), ALU.mult).then_inc(yn_ready, 1)
                dve.wait_ge(out_up, t + 1)
                chained(dve.tensor_tensor(X[:, t, :], X[:, t, :], psY[:, 256:256 + C], ALU.add), STATS + t * DVE_STEPS + 2)

            norm(0)
            rope(0, 0)
            with dve.Fori(0, BATCH) as b:
                for i in range(TILES):
                    t = b * TILES + i
                    norm(b * TILES + (i + 1))
                    maxima(t, i % 2)
                    rope(b * TILES + (i + 1), (i + 1) % TILES)
                    out(t)

        @block.tensor
        def _(pe):
            pe.wait_ge(start, 7)

            def front_x(t, i):
                pe.wait_ge(xn_ready, t + 1)
                pe.transpose(psT[:, 0:P], xn[:], K["ident"][:]).then_inc(xT_up, 1)

            def front_qkv(t, i):
                pe.wait_ge(xT_ready, t + 1)
                pe.wait_ge(rope_ready, t * 3)
                pe.wait_ge(v_ready, t)
                own = xnT[:, PAD + i * P:PAD + (i + 1) * P]
                pe.matmul(psA[:, 0:256], own, W["qkvT"][:, 0:256], start=True, stop=True)
                pe.matmul(psA[:, 256:384], xnT[:, i * P:(i + 1) * P], W["qkvT"][:, 256:384], start=True, stop=True)
                pe.matmul(psA[:, 384:512], own, W["qkvT"][:, 256:384], start=True, stop=True).then_inc(qkv_up, 1)

            def front_stacks(t, i):
                s = i % 2
                pe.wait_ge(lo_ready, (t + 1) * 2)
                for g in range(HG):
                    pe.transpose(psD[:, g, :], qs[:, s, g * P:(g + 1) * P], K["ident16"][:])
                    last = pe.transpose(psD[:, HG + g, :], ks[:, s, g * P:(g + 1) * P], K["ident16"][:])
                last.then_inc(st_up, 1)

            def scores1(t, i):
                pe.wait_ge(qkT_ready, t + 1)
                first = 0 if i == 0 else 1
                for r in range(HG):
                    pe.wait_ge(p_ready, t * HG)
                    pe.matmul(psS[r][:], K["ident_bf"][:],
                              K["mask_q"][:, first, :].unsqueeze(1).broadcast_to([P, HG, P]), start=True, stop=True)
                    for g in range(HG):
                        for j in range(2):
                            w = 2 * i + j
                            last = pe.matmul(psS[r][QB * j:QB * (j + 1), g * P:(g + 1) * P],
                                             qkT[ROWS * r:ROWS * r + 24, g, PAD + QB * w:PAD + QB * (w + 1)],
                                             qkT[ROWS * r:ROWS * r + 24, HG + g, QB * w:QB * w + P],
                                             start=False, stop=True, skip_group_check=True)
                    last.then_inc(s1_up, 1)

            def turn_q2(t, i):
                s = i % 2
                pe.wait_ge(m_ready, t + 1)
                pe.wait_ge(qkT_ready, t + 1)
                for g in range(HG):
                    last = pe.transpose(psD[:, g, :], qs[:, s, g * P:(g + 1) * P], K["ident16"][:])
                last.then_inc(q2_up, 1)

            def scores2(t, i):
                pe.wait_ge(q2_ready, t + 1)
                first = 0 if i == 0 else 1
                for r in range(HG):
                    pe.wait_ge(s1_used, t * HG + (r + 1))
                    pe.matmul(psS[r][:], K["ident_bf"][:],
                              K["mask_k"][:, first, :].unsqueeze(1).broadcast_to([P, HG, P]), start=True, stop=True)
                    for g in range(HG):
                        for j in range(2):
                            w = 2 * i + j
                            last = pe.matmul(psS[r][:, g * P + QB * j:g * P + QB * (j + 1)],
                                             qkT[ROWS * r:ROWS * r + 25, HG + g, QB * w:QB * w + P],
                                             q2T[ROWS * r:ROWS * r + 25, g, QB * j:QB * (j + 1)],
                                             start=False, stop=True, skip_group_check=True)
                    last.then_inc(s2_up, 1)

            def values(t, i):
                pe.wait_ge(v_ready, t + 1)
                pe.wait_ge(dve_step, STATS + t * DVE_STEPS)
                for r in range(HG):
                    pe.wait_ge(p_ready, t * HG + (r + 1))
                    for g in range(HG):
                        for j in range(2):
                            h = HG * g + r
                            last = pe.matmul(psY[QB * j:QB * (j + 1), h * (D + 1):(h + 1) * (D + 1)],
                                             prob[:, r, g * P + QB * j:g * P + QB * (j + 1)],
                                             v_sb[:, 2 * i + j, h, :], start=True, stop=True)
                last.then_inc(pv_up, 1)

            def out(t):
                pe.wait_ge(yn_ready, t + 1)
                pe.wait_ge(xT_ready, t + 2)
                pe.transpose(psT[:, 0:P], yn[:], K["ident"][:]).then_inc(yT_up, 1)
                pe.wait_ge(yT_ready, t + 1)
                pe.matmul(psY[:, 256:256 + C], yT[:], W["projT"][:], start=True, stop=True).then_inc(out_up, 1)

            front_x(0, 0)
            front_qkv(0, 0)
            front_stacks(0, 0)
            with pe.Fori(0, BATCH) as b:
                for i in range(TILES):
                    t = b * TILES + i
                    n, m = b * TILES + (i + 1), (i + 1) % TILES
                    scores1(t, i)
                    front_x(n, m)
                    front_qkv(n, m)
                    turn_q2(t, i)
                    scores2(t, i)
                    front_stacks(n, m)
                    values(t, i)
                    out(t)


def mixture(nc, sb, psum, sem, X, K, W, tag):
    st = sb(tag + "st", [P, TILES, 6], F32)
    mv = sb(tag + "mv", [P, TILES, 2], F32)
    rstd = sb(tag + "rstd", [P, TILES, 1], F32)
    tmp = sb(tag + "tmp", [P, TILES], F32)
    xn = sb(tag + "xn", [P, TILES, C], F32)
    xnT = sb(tag + "xnT", [P, T], F32)
    pad = sb(tag + "pad", [P, 1], F32)
    lg = sb(tag + "lg", [P, TILES, E], F32)
    top = sb(tag + "top", [P, TILES, 8], F32)
    idx = sb(tag + "idx", [P, TILES, 8], U32)
    idf = sb(tag + "idf", [P, TILES, 2], F32)
    gap = sb(tag + "gap", [P, TILES], F32)
    th = sb(tag + "th", [P, TILES], F32)
    w12 = sb(tag + "w12", [P, TILES, 2], F32)
    pick = sb(tag + "pick", [P, TILES, 2, E], F32)
    gate = sb(tag + "gate", [P, 2, TILES, E], F32)
    su = sb(tag + "su", [P, 2, T], F32)
    hid = sb(tag + "hid", [P, 4, T], F32)

    psU = [psum(f"{tag}psU{i}", [P, 512], F32) for i in range(2)]
    psV = [psum(f"{tag}psV{i}", [P, 512], F32) for i in range(2)]
    psY = [psum(f"{tag}psY{i}", [P, 512], F32) for i in range(2)]
    psT = psum(tag + "psT", [P, 512], F32)
    psL = psum(tag + "psL", [P, 512], F32)

    xn_ready = sem(tag + "xn_ready")
    xT_up = sem(tag + "xT_up")
    xT_ready = sem(tag + "xT_ready")
    lg_up = sem(tag + "lg_up")
    gap_ready = sem(tag + "gap_ready")
    th_ready = sem(tag + "th_ready")
    u_up = sem(tag + "u_up")
    v_up = sem(tag + "v_up")
    su_ready = sem(tag + "su_ready")
    h_ready = sem(tag + "h_ready")
    y_up = sem(tag + "y_up")
    y_used = sem(tag + "y_used")
    dve_step = sem(tag + "dve_step")
    FRONT = 2 + RSQRT_LINKS + 8
    UNITS = E * HC

    with nc.Block() as block:

        @block.vector
        def _(dve):
            dve.sem_inc(h_ready, 2)
            dve.sem_inc(y_used, 2)

            def chained(ins, value, n=1):
                if n:
                    ins.then_inc(dve_step, 1)
                dve.wait_ge(dve_step, value)

            def front(b):
                s0 = b * FRONT
                for i in range(TILES):
                    ins = dve.bn_stats(st[:, i, :], X[:, b * TILES + i, :])
                chained(ins, s0 + 1)
                dve.memset(pad[:], 0.0)
                for i in range(TILES):
                    ins = dve.bn_aggr(mv[:, i, :], st[:, i, :])
                chained(ins, s0 + 2)
                rsqrt(dve, chained, mv[:, :, 1], rstd[:, :, 0], tmp[:], s0 + 2)
                for i in range(TILES):
                    dve.wait_ge(xT_up, b)
                    ins = dve.tensor_scalar(xn[:, i, :], X[:, b * TILES + i, :], mv[:, i, 0:1], rstd[:, i, :],
                                            ALU.subtract, ALU.mult)
                ins.then_inc(xn_ready, 1)

            def gates(b, slot):
                s0 = b * FRONT + 2 + RSQRT_LINKS
                dve.wait_ge(lg_up, b + 1)
                chained(dve.tensor_copy(lg[:], psL[:, 0:TILES * E].rearrange("p (i e) -> p i e", e=E)), s0 + 1)
                dve.memset(pad[:], 0.0)
                for i in range(TILES):
                    ins = dve.max(top[:, i, :], lg[:, i, :])
                chained(ins, s0 + 2)
                dve.tensor_tensor(gap[:], top[:, :, 0], top[:, :, 1], ALU.subtract).then_inc(gap_ready, 1)
                for i in range(TILES):
                    ins = dve.max_index(idx[:, i, :], top[:, i, :], lg[:, i, :])
                chained(ins, s0 + 3)
                chained(dve.tensor_copy(idf[:], idx[:, :, 0:2]), s0 + 4)
                dve.wait_ge(th_ready, b + 1)
                chained(dve.tensor_scalar(w12[:, :, 0], th[:], 0.5, 0.5, ALU.mult, ALU.add), s0 + 5)
                chained(dve.tensor_scalar(w12[:, :, 1], th[:], -0.5, 0.5, ALU.mult, ALU.add), s0 + 6)
                for i in range(TILES):
                    for k in range(2):
                        ins = dve.tensor_scalar(pick[:, i, k, :], K["iota"][:], idf[:, i, k:k + 1], w12[:, i, k:k + 1],
                                                ALU.is_equal, ALU.mult)
                chained(ins, s0 + 7)
                chained(dve.tensor_tensor(gate[:, slot, :, :], pick[:, :, 0, :], pick[:, :, 1, :], ALU.add), s0 + 8)

            def collect(b, e, slot):
                dve.wait_ge(y_up, b * E + (e + 1))
                dve.wait_ge(y_used, b * E + (e + 2))
                for i in range(TILES):
                    ins = dve.scalar_tensor_tensor(X[:, b * TILES + i, :], psY[e % 2][:, i * P:(i + 1) * P],
                                                   gate[:, slot, i, e:e + 1], X[:, b * TILES + i, :],
                                                   ALU.mult, ALU.add)
                ins.then_inc(y_used, 1)

            front(0)
            gates(0, 0)
            with dve.Fori(0, BATCH // 2) as b2:
                for half in range(2):
                    b = b2 * 2 + half
                    for e in range(E):
                        for c in range(HC):
                            n = e * HC + c
                            dve.wait_ge(su_ready, b * UNITS + (n + 1))
                            dve.wait_ge(v_up, b * UNITS + (n + 1))
                            if e >= 2:
                                dve.wait_ge(y_up, b * E + (e - 1))
                            dve.tensor_tensor(hid[:, n % 4, :], su[:, n % 2, :], psV[n % 2][:],
                                              ALU.mult).then_inc(h_ready, 1)
                        if e >= 1:
                            collect(b, e - 1, half)
                    front(b2 * 2 + (half + 1))
                    gates(b2 * 2 + (half + 1), (half + 1) % 2)
                    collect(b, E - 1, half)

        @block.scalar
        def _(act):
            def front(b):
                act.wait_ge(xT_up, b + 1)
                act.copy(xnT[:], psT[:]).then_inc(xT_ready, 1)
                act.wait_ge(gap_ready, b + 1)
                act.activation(th[:], gap[:], ACT.Tanh, scale=0.5).then_inc(th_ready, 1)

            front(0)
            with act.Fori(0, BATCH) as b:
                for n in range(UNITS):
                    act.wait_ge(u_up, b * UNITS + (n + 1))
                    act.wait_ge(h_ready, b * UNITS + (n + 1))
                    act.activation(su[:, n % 2, :], psU[n % 2][:], ACT.Silu).then_inc(su_ready, 1)
                front(b + 1)

        @block.tensor
        def _(pe):
            def front(b):
                pe.wait_ge(xn_ready, b + 1)
                for i in range(TILES):
                    ins = pe.transpose(psT[:, i * P:(i + 1) * P], xn[:, i, :], K["ident"][:])
                ins.then_inc(xT_up, 1)
                pe.wait_ge(xT_ready, b + 1)
                for i in range(TILES):
                    ins = pe.matmul(psL[:, i * E:(i + 1) * E], xnT[:, i * P:(i + 1) * P], W["g"][:], start=True, stop=True)
                ins.then_inc(lg_up, 1)

            def up(b, e):
                for c in range(HC):
                    n = e * HC + c
                    if n >= 2:
                        pe.wait_ge(su_ready, b * UNITS + (n - 1))
                    pe.matmul(psU[n % 2][:], W["w1"][:, e, c * P:(c + 1) * P], xnT[:], start=True, stop=True).then_inc(u_up, 1)
                    pe.wait_ge(h_ready, b * UNITS + (n + 1))
                    pe.matmul(psV[n % 2][:], W["w2"][:, e, c * P:(c + 1) * P], xnT[:], start=True, stop=True).then_inc(v_up, 1)

            def down(b, e):
                pe.wait_ge(h_ready, b * UNITS + (2 + (e + 1) * HC))
                pe.wait_ge(y_used, b * E + (e + 1))
                for i in range(TILES):
                    for c in range(HC):
                        ins = pe.matmul(psY[e % 2][:, i * P:(i + 1) * P], hid[:, (e * HC + c) % 4, i * P:(i + 1) * P],
                                        W["w3"][:, e, c, :], start=(c == 0), stop=(c == HC - 1))
                ins.then_inc(y_up, 1)

            front(0)
            with pe.Fori(0, BATCH) as b:
                for e in range(E):
                    up(b, e)
                    if e >= 1:
                        down(b, e - 1)
                front(b + 1)
                down(b, E - 1)


def scan(nc, sb, psum, sem, X, K, W):
    pad = sb("s_pad", [P, 1], F32)
    st = sb("s_st", [P, TILES, 6], F32)
    mv = sb("s_mv", [P, TILES, 2], F32)
    rstd = sb("s_rstd", [P, TILES, 1], F32)
    tmp = sb("s_tmp", [P, TILES], F32)
    xn = sb("s_xn", [P, TILES, C], F32)
    xnT = sb("s_xnT", [P, 2, T], F32)
    rT = sb("s_rT", [RANK, T], F32)
    ez = sb("s_ez", [P, T], F32)
    lp = sb("s_lp", [P, T], F32)
    dlt = sb("s_dlt", [P, T], F32)
    dx = sb("s_dx", [P, T], F32)
    halves = sb("s_halves", [P, 2, 4, T], F16)
    Brep = sb("s_Brep", [P, 2, T], F32)
    Crep = sb("s_Crep", [P, 2, T], F32)
    abar = sb("s_abar", [P, 2, T], F32)
    dbx = sb("s_dbx", [P, 2, T], F32)
    hst = sb("s_hst", [P, 4, T], F32)
    hc = sb("s_hc", [P, 2, T], F32)
    yT = sb("s_yT", [P, T], F32)

    psE = [psum(f"s_psE{i}", [P, 512], F32) for i in range(2)]
    psX = [psum(f"s_psX{i}", [P, 512], F32) for i in range(2)]
    psY = psum("s_psY", [P, 512], F32)
    psT = psum("s_psT", [P, 512], F32)
    psR = psum("s_psR", [P, 512], F32)
    psO = psum("s_psO", [P, 512], F32)

    xn_ready = sem("s_xn_ready")
    xT_up = sem("s_xT_up")
    xT_ready = sem("s_xT_ready")
    proj_up = sem("s_proj_up")
    proj_used = sem("s_proj_used")
    ez_ready = sem("s_ez_ready")
    halves_ready = sem("s_halves_ready")
    e_up = sem("s_e_up")
    x_up = sem("s_x_up")
    a_ready = sem("s_a_ready")
    dbx_ready = sem("s_dbx_ready")
    h_ready = sem("s_h_ready")
    hc_ready = sem("s_hc_ready")
    hc_used = sem("s_hc_used")
    y_up = sem("s_y_up")
    y_ready = sem("s_y_ready")
    o_up = sem("s_o_up")
    dve_step = sem("s_dve_step")
    FRONT = 2 + RSQRT_LINKS
    STEPS = FRONT + 10
    x_done = sem("s_x_done")

    with nc.Block() as block:

        @block.vector
        def _(dve):
            dve.sem_inc(h_ready, 3)
            dve.sem_inc(dbx_ready, 2)

            def chained(ins, value):
                ins.then_inc(dve_step, 1)
                dve.wait_ge(dve_step, value)

            def front(b, slot):
                s0 = b * STEPS
                for i in range(TILES):
                    ins = dve.bn_stats(st[:, i, :], X[:, b * TILES + i, :])
                chained(ins, s0 + 1)
                dve.memset(pad[:], 0.0)
                for i in range(TILES):
                    ins = dve.bn_aggr(mv[:, i, :], st[:, i, :])
                chained(ins, s0 + 2)
                rsqrt(dve, chained, mv[:, :, 1], rstd[:, :, 0], tmp[:], s0 + 2)
                dve.wait_ge(xT_up, b)
                for i in range(TILES):
                    ins = dve.tensor_scalar(xn[:, i, :], X[:, b * TILES + i, :], mv[:, i, 0:1], rstd[:, i, :],
                                            ALU.subtract, ALU.mult)
                ins.then_inc(xn_ready, 1)

            def deltas(b, slot):
                s0 = b * STEPS + FRONT
                dve.wait_ge(ez_ready, b + 1)
                chained(dve.tensor_scalar(ez[:], ez[:], E_MAX, None, ALU.min), s0 + 1)
                chained(dve.tensor_scalar(lp[:], ez[:], float(LOG_POLY[5]), None, ALU.mult), s0 + 2)
                for n, k in enumerate((4, 3, 2, 1, 0)):
                    chained(dve.scalar_tensor_tensor(lp[:], lp[:], float(LOG_POLY[k]), ez[:], ALU.add, ALU.mult), s0 + 3 + n)
                chained(dve.tensor_scalar(dlt[:], lp[:], DT_MIN, DT_MAX, ALU.max, ALU.min), s0 + 8)
                chained(dve.tensor_tensor(dx[:], dlt[:], xnT[:, slot, :], ALU.mult), s0 + 9)
                dve.wait_ge(y_up, b)
                dve.tensor_scalar(halves[:, slot, 0, :], dlt[:], UP, None, ALU.mult)
                chained(dve.tensor_scalar(halves[:, slot, 2, :], dx[:], UP, None, ALU.mult), s0 + 10)
                dve.scalar_tensor_tensor(halves[:, slot, 1, :], dlt[:], UP, halves[:, slot, 0, :], ALU.mult, ALU.subtract)
                dve.scalar_tensor_tensor(halves[:, slot, 3, :], dx[:], UP, halves[:, slot, 2, :],
                                         ALU.mult, ALU.subtract).then_inc(halves_ready, 1)

            def drive(b, g, slot):
                dve.wait_ge(x_up, b * G + (g + 1))
                dve.wait_ge(h_ready, b * G + (g + 2))
                dve.tensor_tensor(dbx[:, g % 2, :], psX[g % 2][:], Brep[:, slot, :], ALU.mult).then_inc(dbx_ready, 1)

            def states(b, g):
                dve.wait_ge(a_ready, b * G + (g + 1))
                dve.wait_ge(dbx_ready, b * G + (g + 3))
                dve.wait_ge(hc_ready, b * G + g)
                dve.tensor_tensor_scan(hst[:, g % 4, :], abar[:, g % 2, :], dbx[:, g % 2, :], 0.0,
                                       ALU.mult, ALU.add).then_inc(h_ready, 1)

            front(0, 0)
            deltas(0, 0)
            with dve.Fori(0, BATCH // 2) as b2:
                for half in range(2):
                    b = b2 * 2 + half
                    dve.wait_ge(proj_used, (b + 1) * 4)
                    for g in range(G):
                        drive(b, g, half)
                        if g >= 1:
                            states(b, g - 1)
                    states(b, G - 1)
                    front(b2 * 2 + (half + 1), (half + 1) % 2)
                    deltas(b2 * 2 + (half + 1), (half + 1) % 2)
                    dve.wait_ge(y_up, b + 1)
                    dve.scalar_tensor_tensor(yT[:], xnT[:, half, :], W["D"][:], psY[:], ALU.mult, ALU.add).then_inc(y_ready, 1)
                    dve.wait_ge(o_up, b + 1)
                    dve.tensor_tensor(X[:, bass.ds(b * TILES, TILES), :], X[:, bass.ds(b * TILES, TILES), :],
                                      psO[:].rearrange("p (i c) -> p i c", c=C), ALU.add).then_inc(x_done, 1)

        @block.gpsimd
        def _(pool):
            pool.sem_inc(hc_ready, 2)
            with pool.Fori(0, BATCH // 2) as b2:
                for half in range(2):
                    b = b2 * 2 + half
                    for g in range(G):
                        pool.wait_ge(h_ready, b * G + (g + 4))
                        pool.wait_ge(hc_used, b * G + (g + 1))
                        pool.tensor_tensor(hc[:, g % 2, :], hst[:, g % 4, :], Crep[:, half, :], ALU.mult).then_inc(hc_ready, 1)

        @block.scalar
        def _(act):
            def front(b, slot):
                act.wait_ge(xT_up, b + 1)
                act.copy(xnT[:, slot, :], psT[:]).then_inc(xT_ready, 1)
                act.wait_ge(proj_up, b * 4 + 1)
                act.copy(rT[:], psR[0:RANK, :]).then_inc(proj_used, 1)
                act.wait_ge(proj_up, b * 4 + 2)
                act.activation(ez[:], psR[:], ACT.Exp, bias=W["dtb"][:]).then_inc(ez_ready, 1)
                act.wait_ge(ez_ready, b + 1)
                act.sem_inc(proj_used, 1)
                act.wait_ge(proj_up, b * 4 + 3)
                act.mul(Brep[:, slot, :], psR[:], 1.0 / UP).then_inc(proj_used, 1)
                act.wait_ge(proj_up, b * 4 + 4)
                act.copy(Crep[:, slot, :], psR[:]).then_inc(proj_used, 1)

            front(0, 0)
            with act.Fori(0, BATCH // 2) as b2:
                for half in range(2):
                    b = b2 * 2 + half
                    for g in range(G):
                        act.wait_ge(e_up, b * G + (g + 1))
                        act.wait_ge(h_ready, b * G + (g + 2))
                        act.activation(abar[:, g % 2, :], psE[g % 2][:], ACT.Exp, scale=W["A"][:, g:g + 1]).then_inc(a_ready, 1)
                    front(b2 * 2 + (half + 1), (half + 1) % 2)

        @block.tensor
        def _(pe):
            pe.sem_inc(hc_used, 2)

            def front(b, slot):
                pe.wait_ge(xn_ready, b + 1)
                for i in range(TILES):
                    ins = pe.transpose(psT[:, i * P:(i + 1) * P], xn[:, i, :], K["ident"][:])
                ins.then_inc(xT_up, 1)
                pe.wait_ge(xT_ready, b + 1)
                pe.matmul(psR[0:RANK, :], W["xpT"][:], xnT[:, slot, :], start=True, stop=True).then_inc(proj_up, 1)
                pe.wait_ge(proj_used, b * 4 + 1)
                pe.matmul(psR[:], W["dtT"][:], rT[:], start=True, stop=True).then_inc(proj_up, 1)
                pe.wait_ge(proj_used, b * 4 + 2)
                pe.matmul(psR[:], W["BT"][:], xnT[:, slot, :], start=True, stop=True).then_inc(proj_up, 1)
                pe.wait_ge(proj_used, b * 4 + 3)
                pe.matmul(psR[:], W["CT"][:], xnT[:, slot, :], start=True, stop=True).then_inc(proj_up, 1)

            def spread(b, g, slot):
                sel = K["sel"][:, g * P:(g + 1) * P]
                if g >= 2:
                    pe.wait_ge(a_ready, b * G + (g - 1))
                pe.matmul(psE[g % 2][:], sel, halves[:, slot, 0, :], start=True, stop=False)
                pe.matmul(psE[g % 2][:], sel, halves[:, slot, 1, :], start=False, stop=True).then_inc(e_up, 1)
                pe.wait_ge(dbx_ready, b * G + (g + 1))
                pe.matmul(psX[g % 2][:], sel, halves[:, slot, 2, :], start=True, stop=False)
                pe.matmul(psX[g % 2][:], sel, halves[:, slot, 3, :], start=False, stop=True).then_inc(x_up, 1)

            def gather(b, g):
                pe.wait_ge(hc_ready, b * G + (g + 3))
                pe.matmul(psY[:], K["selT"][:, g * P:(g + 1) * P], hc[:, g % 2, :], start=(g == 0),
                          stop=(g == G - 1)).then_inc(hc_used, 1)

            front(0, 0)
            with pe.Fori(0, BATCH // 2) as b2:
                for half in range(2):
                    b = b2 * 2 + half
                    pe.wait_ge(halves_ready, b + 1)
                    pe.wait_ge(y_ready, b)
                    for g in range(G):
                        spread(b, g, half)
                        if g >= 2:
                            gather(b, g - 2)
                    gather(b, G - 2)
                    gather(b, G - 1)
                    pe.wait_ge(hc_used, (b + 1) * G + 2)
                    pe.sem_inc(y_up, 1)
                    front(b2 * 2 + (half + 1), (half + 1) % 2)
                    pe.wait_ge(y_ready, b + 1)
                    for i in range(TILES):
                        ins = pe.transpose(psO[:, i * P:(i + 1) * P], yT[:, i * P:(i + 1) * P], K["ident"][:])
                    ins.then_inc(o_up, 1)


def build(nc, x_in, x_out, dram, phases=4):
    with ExitStack() as outer:
        def keep(name, shape, dt):
            return outer.enter_context(nc.sbuf_tensor(name, shape, dt))

        def sem(name):
            return outer.enter_context(nc.semaphore(name))

        X = keep("X", [P, NT + TILES, C], F32)
        K = {n: keep("k_" + n, list(s), dt) for n, s, dt in (
            ("ident", (P, P), F32), ("ident16", (P, P), F16), ("masks", (P, 2, 2, P), F32),
            ("cos", (P, TILES, 4), F32), ("sin", (P, TILES, 4), F32), ("nsin", (P, TILES, 4), F32),
            ("iota", (P, E), F32), ("sel", (P, G * P), F16), ("selT", (P, G * P), F32))}
        ident_bf = keep("ident_bf", [P, P], BF16)
        masks_bf = keep("masks_bf", [P, 2, 2, P], BF16)
        W = {n: keep("w_" + n, list(s), F32) for n, s in (
            ("qkvT", (P, 3 * C)), ("projT", (P, C)), ("g", (P, E)), ("w1", (P, E, HID)), ("w2", (P, E, HID)),
            ("w3", (P, E, HC, C)), ("A", (P, G)), ("D", (P, 1)), ("dtb", (P, 1)), ("xpT", (P, RANK)),
            ("dtT", (RANK, P)), ("BT", (P, P)), ("CT", (P, P)))}
        loaded = sem("loaded")
        a_step = sem("a_log_step")
        with nc.Block() as block:
            xin = x_in.rearrange("(t p) c -> p t c", p=P)
            n_loads = [0]

            @block.sync
            def _(sp):
                for q in range(4):
                    sp.dma_start(X[:, q * 8:(q + 1) * 8, :], xin[:, q * 8:(q + 1) * 8, :]).then_inc(loaded, 16)
                    n_loads[0] += 1
                for n in ("w1", "w2", "w3"):
                    sp.dma_start(W[n][:], dram[n]).then_inc(loaded, 16)
                    n_loads[0] += 1
                for n in K:
                    sp.dma_start(K[n][:], dram[n]).then_inc(loaded, 16)
                    n_loads[0] += 1
                for n in ("qkvT", "projT", "g", "A", "D", "dtb", "xpT", "dtT", "BT", "CT"):
                    sp.dma_start(W[n][:], dram[n]).then_inc(loaded, 16)
                    n_loads[0] += 1
                sp.wait_ge(loaded, 16 * n_loads[0])

            @block.scalar
            def _(act):
                act.wait_ge(loaded, 16 * n_loads[0])
                act.activation(W["A"][:], W["A"][:], ACT.Exp).then_inc(a_step, 1)

            @block.vector
            def _(dve):
                dve.memset(X[:, NT:NT + TILES, :], 0.0).then_inc(a_step, 1)
                dve.wait_ge(a_step, 2)
                dve.tensor_scalar(W["A"][:], W["A"][:], -1.0 / UP, None, ALU.mult).then_inc(a_step, 1)
                dve.wait_ge(loaded, 16 * n_loads[0])
                dve.tensor_copy(ident_bf[:], K["ident"][:]).then_inc(a_step, 1)
                dve.tensor_copy(masks_bf[:], K["masks"][:]).then_inc(a_step, 1)
                dve.wait_ge(a_step, 5)

        K["ident_bf"] = ident_bf
        K["mask_q"], K["mask_k"] = masks_bf[:, 0], masks_bf[:, 1]

        def stage(n, fn, *args):
            if phases < n:
                return
            with ExitStack() as ctx:
                def sb(name, shape, dt):
                    return ctx.enter_context(nc.sbuf_tensor(name, shape, dt))

                def psum(name, shape, dt):
                    return ctx.enter_context(nc.psum_tensor(name, shape, dt))
                fn(nc, sb, psum, sem, X, K, W, *args)

        stage(1, attention)
        stage(2, mixture, "f_")
        stage(3, scan)
        stage(4, mixture, "g_")

        stored = sem("stored")
        with nc.Block() as block:
            @block.sync
            def _(sp):
                xo = x_out.rearrange("(t p) c -> p t c", p=P)
                for q in range(4):
                    sp.dma_start(xo[:, q * 8:(q + 1) * 8, :], X[:, q * 8:(q + 1) * 8, :]).then_inc(stored, 16)
                sp.wait_ge(stored, 64)


def constants():
    f = np.float32
    inv = (1.0 / np.float32(10000.0) ** (np.arange(0, D, 2, dtype=f) / f(D))).astype(f)
    ang = np.outer(np.arange(T, dtype=f), inv).astype(f).reshape(TILES, P, 4).transpose(1, 0, 2)
    p = np.arange(P)[:, None]
    k = np.arange(P)[None, :]
    q = p % QB
    ok = (k >= q) & (k <= q + QB)
    ok0 = ok & ((k >= QB) | (p >= QB))
    mask_q = np.stack([ok0, ok], 1)
    kk, col = p, k
    okk = (kk >= col % QB) & (kk <= col % QB + QB)
    okk0 = okk & ((kk >= QB) | (col >= QB))
    mask_k = np.stack([okk0, okk], 1)
    NEG = -1e30
    sel = np.zeros((P, G, P), f)
    for g in range(G):
        for r in range(P):
            sel[DG * g + r // NS, g, r] = 1
    return {
        "ident": np.eye(P, dtype=f), "ident16": np.eye(P, dtype=np.float16),
        "masks": np.stack([np.where(m, 0, NEG) for m in (mask_q, mask_k)], 1).astype(f),
        "cos": np.cos(ang).astype(f), "sin": np.sin(ang).astype(f), "nsin": (-np.sin(ang)).astype(f),
        "iota": np.tile(np.arange(E, dtype=f), (P, 1)),
        "sel": sel.reshape(P, G * P).astype(np.float16),
        "selT": np.ascontiguousarray(sel.transpose(2, 1, 0)).reshape(P, G * P),
    }


PHASES = 4


def kernel(**inputs):
    import concourse.bacc as bacc
    from concourse.bass_utils import run_bass_kernel_spmd

    a = {n: np.asarray(v) for n, v in inputs.items()}
    lay = {
        "x": a["L0_attn_a_x"].reshape(BATCH * T, C),
        "qkvT": a["L0_attn_a_w_attn"].T, "projT": a["L0_attn_a_w_proj"].T,
        "g": a["L0_ffn_Wg"],
        "w1": a["L0_ffn_W1"].transpose(1, 0, 2), "w2": a["L0_ffn_W2"].transpose(1, 0, 2),
        "w3": a["L0_ffn_W3"].reshape(E, HC, P, C).transpose(2, 0, 1, 3),
        "A": a["L0_attn_b_A_log"].reshape(G, DG * NS).T,
        "D": a["L0_attn_b_D"].reshape(P, 1), "dtb": a["L0_attn_b_dt_proj_b"].reshape(P, 1),
        "xpT": a["L0_attn_b_x_proj_w"].T, "dtT": a["L0_attn_b_dt_proj_w"].T,
        "BT": np.tile(a["L0_attn_b_B_proj_w"].T, (1, DG)), "CT": np.tile(a["L0_attn_b_C_proj_w"].T, (1, DG)),
    }
    lay.update(constants())
    arrays = {n + "_dram": np.ascontiguousarray(v) for n, v in lay.items()}
    nc = bacc.Bacc("TRN2", target_bir_lowering=False, num_devices=1)
    dram = {n[:-5]: nc.dram_tensor(n, v.shape, mybir.dt.from_np(v.dtype), kind="ExternalInput").ap() for n, v in arrays.items()}
    out = nc.dram_tensor("out_dram", (BATCH * T, C), F32, kind="ExternalOutput").ap()
    build(nc, dram["x"], out, dram, PHASES)
    r = run_bass_kernel_spmd(nc, [arrays], core_ids=[0])
    return r.results[0]["out_dram"].reshape(BATCH, T, C)
```

```python
from contextlib import ExitStack

import numpy as np

import concourse.bass as bass
from concourse import mybir

ALU = mybir.AluOpType
ACT = mybir.ActivationFunctionType
AX_X = mybir.AxisListType.X
F32 = mybir.dt.float32
F16 = mybir.dt.float16
BF16 = mybir.dt.bfloat16
U32 = mybir.dt.uint32
I32 = mybir.dt.int32

P = 128
BATCH, T, C = 8, 512, 128
TILES = T // P
NT = BATCH * TILES
H, D = 16, 8
WINDOW = 64
QB = WINDOW
HG = 4
ROWS = 32
E, HID = 8, 256
HC = HID // P
NS = 16
DG = P // NS
G = C // DG
QUARTER, QUARTERS = 32, C // 32
SUBS = G // QUARTERS
RANK = 64
EPS = 1e-5
DT_MIN, DT_MAX = 0.001, 0.1
UP = 1024.0
W_UP = {"w1": 16.0, "w2": 8.0, "w3": 16.0}
Y_UP = W_UP["w2"] * W_UP["w3"]
E_MAX = 0.1052
LOG_POLY = np.polynomial.chebyshev.Chebyshev.interpolate(
    lambda e: np.log1p(e) / e, 5, domain=[1e-9, E_MAX]).convert(kind=np.polynomial.Polynomial).coef


RSQRT_LINKS = 12
MOMENT_LINKS = 1 + RSQRT_LINKS
STAT_LINKS = 2 * MOMENT_LINKS


def rsqrt(dve, chained, v, y, t, first):
    chained(dve.tensor_scalar(v, v, EPS, None, ALU.add), first + 1)
    chained(dve.tensor_scalar(t.bitcast(I32), v.bitcast(I32), 1, None, ALU.logical_shift_right), first + 2)
    dve.tensor_scalar(y.bitcast(I32), t.bitcast(I32), -1.0, float(0x5F3759DF), ALU.mult, ALU.add)
    chained(dve.tensor_scalar(v, v, -0.5, None, ALU.mult), first + 3)
    for k in range(3):
        chained(dve.tensor_tensor(t, y, y, ALU.mult), first + 4 + 3 * k)
        chained(dve.tensor_tensor(t, t, v, ALU.mult), first + 5 + 3 * k)
        chained(dve.scalar_tensor_tensor(y, t, 1.5, y, ALU.add, ALU.mult), first + 6 + 3 * k)


def moments(dve, chained, st, mv, rstd, tmp, t0, end, link):
    for t in range(t0, min(end, NT)):
        ins = dve.bn_aggr(mv[:, t, :], st[:, t, :])
    chained(ins, link + 1)
    rsqrt(dve, chained, mv[:, t0:end, 1], rstd[:, t0:end, 0], tmp[:, t0:end], link + 1)


def attention(nc, sb, psum, sem, X, K, W, x_in, dram, groups, loaded, st_out):
    assert E == BATCH
    PAD = QB
    PART = NT // 4
    AHEAD = TILES
    st = sb("a_st", [P, NT, 6], F32)
    mv = sb("a_mv", [P, NT + AHEAD, 2], F32)
    rstd = sb("a_rstd", [P, NT + AHEAD, 1], F32)
    tmp = sb("a_tmp", [P, NT + AHEAD], F32)
    pad = sb("a_pad", [P, 1], F32)
    xn = sb("a_xn", [P, C], F32)
    xnT = sb("a_xnT", [P, PAD + T], F32)
    rot_cos = sb("a_rot_cos", [P, 2 * C], F32)
    rot_sin = sb("a_rot_sin", [P, 2 * C], F32)
    rot = sb("a_rot", [P, 2 * C], F32)
    qs = sb("a_qs", [P, TILES, H * ROWS], F16)
    ks = sb("a_ks", [P, TILES, H * ROWS], F16)
    qkT = sb("a_qkT", [P, 2 * HG, PAD + T], F16)
    q2T = sb("a_q2T", [P, HG, P], F16)
    v_sb = sb("a_v", [P, 2 * TILES, H, ROWS], F32)
    mx = sb("a_mx", [P, H], F32)
    prob = sb("a_prob", [P, HG, HG * P], F32)
    yc = sb("a_yc", [P, HG * P], F32)
    rden = sb("a_rden", [P, H], F32)
    yn = sb("a_yn", [P, C], F32)
    yT = sb("a_yT", [P, C], F32)

    psS = [psum(f"a_psS{r}", [P, 512], F32) for r in range(HG)]
    psA = psum("a_psA", [P, 512], F32)
    psD = psum("a_psD", [P, 2 * HG, P], F16)
    psT = psum("a_psT", [P, 512], F32)
    psY = psum("a_psY", [P, 512], F32)

    x_first = sem("a_x_first")
    x_rest = sem("a_x_rest")
    made = sem("a_made")
    stats_ready = sem("a_stats_ready")
    psQ = psT[:, 0:HG * P // 2].bitcast(F16).rearrange("p (g q) -> p g q", g=HG)
    start = sem("a_start")
    xn_ready = sem("a_xn_ready")
    xT_up = sem("a_xT_up")
    xT_ready = sem("a_xT_ready")
    qkv_up = sem("a_qkv_up")
    v_ready = sem("a_v_ready")
    rope_ready = sem("a_rope_ready")
    rot_ready = sem("a_rot_ready")
    hi_ready = sem("a_hi_ready")
    lo_ready = sem("a_lo_ready")
    st_up = sem("a_st_up")
    qkT_ready = sem("a_qkT_ready")
    s1_up = sem("a_s1_up")
    s1_used = sem("a_s1_used")
    m_ready = sem("a_m_ready")
    q2_up = sem("a_q2_up")
    q2_ready = sem("a_q2_ready")
    s2_up = sem("a_s2_up")
    p_ready = sem("a_p_ready")
    pv_up = sem("a_pv_up")
    yc_ready = sem("a_yc_ready")
    y_up = sem("a_y_up")
    rden_ready = sem("a_rden_ready")
    yn_ready = sem("a_yn_ready")
    yT_up = sem("a_yT_up")
    yT_ready = sem("a_yT_ready")
    out_up = sem("a_out_up")
    x_done = sem("a_x_done")
    w_high = sem("a_w_high")
    w_low = sem("a_w_low")
    dve_step = sem("a_dve_step")
    HEADS = 24

    def per_head(stack, slot):
        return stack[:, slot, :].rearrange("p (h r) -> p h r", r=ROWS)

    with nc.Block() as block:

        @block.sync
        def _(sp):
            xin = x_in.rearrange("(t p) c -> p t c", p=P)

            def load(group):
                for n in groups[group]:
                    sp.dma_start((K[n] if n in K else W[n])[:], dram[n]).then_inc(loaded[group][0], 16)

            for t in range(0, NT, PART):
                sp.dma_start(X[:, t:t + PART, :], xin[:, t:t + PART, :]).then_inc(x_first if t == 0 else x_rest, 16)
                if t == 0:
                    load("a")
            load("w")
            load("s")

        @block.gpsimd
        def _(pool):
            pool.memset(X[:, NT:, :], 0.0)
            pool.memset(xnT[:, 0:PAD], 0.0).then_inc(start, 1)
            pool.memset(qkT[:, :, 0:PAD], 0.0).then_inc(start, 1)
            pool.memset(v_sb[:], 0.0).then_inc(start, 1)
            pool.memset(qs[:], 0.0).then_inc(start, 1)
            pool.memset(ks[:], 0.0).then_inc(start, 1)
            pool.wait_ge(start, 5)
            pool.memset(v_sb[:, :, :, D:D + 1], 1.0).then_inc(start, 1)
            pool.memset(ks[:].rearrange("p s (h r) -> p (s h) r", r=ROWS)[:, :, HEADS:HEADS + 1], 1.0).then_inc(start, 1)

            def stack(n, i):
                pool.wait_ge(rope_ready, (n + 1) * 3)
                pool.wait_ge(lo_ready, n * 2)
                pool.tensor_tensor(rot[:], rot_cos[:], rot_sin[:], ALU.add).then_inc(rot_ready, 1)
                for half, out in ((0, per_head(qs, i)), (1, per_head(ks, i)[:, :, 0:16])):
                    cos, sin = (x[:, half * C:(half + 1) * C].rearrange("p (h d) -> p h d", d=D).unsqueeze(2)
                                .broadcast_to([P, H, 2, D]) for x in (rot_cos, rot_sin))
                    pool.tensor_tensor(out.rearrange("p h (a d) -> p h a d", a=2)[:, :, :, 0:D], cos, sin,
                                       ALU.add).then_inc(hi_ready, 1)
                pool.wait_ge(rot_ready, n + 1)
                pool.wait_ge(hi_ready, (n + 1) * 2)
                for half, out, lo in ((0, per_head(qs, i), 8), (1, per_head(ks, i), 16)):
                    pool.tensor_tensor(out[:, :, lo:lo + 8], rot[:, half * C:(half + 1) * C].rearrange("p (h d) -> p h d", d=D),
                                       out[:, :, 0:8], ALU.subtract).then_inc(lo_ready, 1)

            def low_weights(e, k, n):
                pool.wait_ge(w_high, e * 3 + (k + 1))
                w, h, lo = (x[:, e].rearrange("p a c -> p (a c)") if n == "w3" else x[:, e, :]
                            for x in (W[n], W[n + "h"], W[n + "l"]))
                pool.tensor_tensor(lo, w, h, ALU.subtract).then_inc(w_low, 1)

            for n in range(3):
                stack(n, n)
            with pool.Fori(0, BATCH) as b:
                for i in range(TILES):
                    stack(b * TILES + (i + 3), (i + 3) % TILES)
                    if i > 0:
                        low_weights(b, i - 1, ("w1", "w2", "w3")[i - 1])
            pool.wait_ge(w_low, 3 * E)

        @block.scalar
        def _(act):
            act.wait_ge(start, 7)

            def turned(n, ni):
                act.wait_ge(xT_up, n + 1)
                act.copy(xnT[:, PAD + ni * P:PAD + (ni + 1) * P], psT[:, 0:P]).then_inc(xT_ready, 1)

            def step(t, i, ends=True, takes=True, scores=True, weights=()):
                c, n, ni, a, ai = t + 1, t + 2, (i + 2) % TILES, t + 3, (i + 3) % TILES

                def exponentials(r):
                    if takes:
                        act.wait_ge(pv_up, c)
                        act.wait_ge(s2_up, c * HG + (r + 1))
                        act.activation(prob[:, r, :], psS[r][:], ACT.Exp, scale=float(D) ** -0.5).then_inc(p_ready, 1)

                if scores:
                    act.wait_ge(st_up, n + 1)
                    act.copy(qkT[:, :, PAD + ni * P:PAD + (ni + 1) * P], psD[:]).then_inc(qkT_ready, 1)
                if weights:
                    high_weights(*weights)
                exponentials(0)
                if ends:
                    act.wait_ge(yT_up, t + 1)
                    act.copy(yT[:], psT[:, 0:P]).then_inc(yT_ready, 1)
                exponentials(1)
                act.wait_ge(rope_ready, (a + 1) * 3)
                act.copy(v_sb[:, 2 * ai:2 * ai + 2, :, 0:D],
                         psA[:, 256:512].rearrange("p (w h d) -> p w h d", w=2, d=D)).then_inc(v_ready, 1)
                exponentials(2)
                exponentials(3)
                turned(a + 1, (ai + 1) % TILES)

            def high_weights(e, n):
                w, h = (x[:, e].rearrange("p a c -> p (a c)") if n == "w3" else x[:, e, :] for x in (W[n], W[n + "h"]))
                act.mul(h, w, W_UP[n])
                act.mul(w, w, W_UP[n]).then_inc(w_high, 1)

            turned(0, 0)
            step(-3, 1, False, False, False)
            step(-2, 2, False, False)
            step(-1, 3, False)
            act.wait_ge(loaded["w"][0], loaded["w"][1])
            with act.Fori(0, BATCH) as b:
                for i in range(TILES):
                    step(b * TILES + i, i, weights=(b, ("w1", "w2", "w3")[i]) if i < 3 else ())

        @block.vector
        def _(dve):
            def chained(ins, value):
                ins.then_inc(dve_step, 1)
                dve.wait_ge(dve_step, value)

            def stats(t0, end):
                for t in range(t0, end):
                    dve.bn_stats(st[:, t, :], X[:, t, :]).then_inc(stats_ready, 1)
                dve.wait_ge(stats_ready, end)

            dve.memset(mv[:, NT:, :], 1.0)
            dve.wait_ge(x_first, 16)
            stats(0, PART)
            dve.memset(pad[:], 0.0)
            moments(dve, chained, st, mv, rstd, tmp, 0, PART, 0)

            def norm(n):
                dve.wait_ge(xT_up, n)
                dve.tensor_scalar(xn[:], X[:, n, :], mv[:, n, 0:1], rstd[:, n, :], ALU.subtract, ALU.mult).then_inc(xn_ready, 1)

            def step(t, i, ends=True, takes=True, scores=True):
                c, n, ni, a, ai = t + 1, t + 2, (i + 2) % TILES, t + 3, (i + 3) % TILES
                if takes:
                    dve.wait_ge(q2_up, c + 1)
                    dve.tensor_copy(q2T[:], psQ).then_inc(q2_ready, 1)
                if ends:
                    y = psY[:].rearrange("p (r g d) -> p g r d", r=HG, d=ROWS)
                    dve.wait_ge(y_up, t + 1)
                    dve.reciprocal(rden[:].rearrange("p (g r) -> p g r", r=HG), y[:, :, :, D]).then_inc(rden_ready, 1)
                    dve.wait_ge(rden_ready, t + 1)
                    dve.wait_ge(yT_up, t)
                    dve.tensor_tensor(yn[:].rearrange("p (g r d) -> p g r d", r=HG, d=D), y[:, :, :, 0:D],
                                      rden[:].rearrange("p (g r) -> p g r", r=HG).unsqueeze(3)
                                      .broadcast_to([P, HG, HG, D]), ALU.mult).then_inc(yn_ready, 1)
                qk = psA[:, 0:256].rearrange("p (h a d) -> p h a d", a=2, d=4)
                crossed = rot_sin[:].rearrange("p (h a d) -> p h a d", a=2, d=4)
                cos = K["cos"][:, ai, :].unsqueeze(1).broadcast_to([P, 4 * H, 4])
                sin = K["sin"][:, ai, :].unsqueeze(1).broadcast_to([P, 2 * H, 4])
                nsin = K["nsin"][:, ai, :].unsqueeze(1).broadcast_to([P, 2 * H, 4])
                dve.wait_ge(qkv_up, a + 1)
                dve.wait_ge(hi_ready, a * 2)
                dve.tensor_tensor(rot_cos[:].rearrange("p (h d) -> p h d", d=4),
                                  psA[:, 0:256].rearrange("p (h d) -> p h d", d=4), cos, ALU.mult).then_inc(rope_ready, 1)
                dve.tensor_tensor(crossed[:, :, 0, :], qk[:, :, 1, :], sin, ALU.mult).then_inc(rope_ready, 1)
                dve.tensor_tensor(crossed[:, :, 1, :], qk[:, :, 0, :], nsin, ALU.mult).then_inc(rope_ready, 1)
                norm(a + 1)
                if ends:
                    dve.wait_ge(out_up, t + 1)
                    dve.tensor_tensor(X[:, t, :], X[:, t, :], psT[:, 0:C], ALU.add).then_inc(x_done, 1)
                if scores:
                    for r in range(HG):
                        dve.wait_ge(s1_up, n * HG + (r + 1))
                        dve.tensor_reduce(mx[:].rearrange("p (g r) -> p g r", r=HG)[:, :, r],
                                          psS[r][:].rearrange("p (g k) -> p g k", g=HG), AX_X, ALU.max).then_inc(s1_used, 1)
                        if ends and r == 0:
                            dve.wait_ge(x_done, t + 1)
                            dve.bn_stats(st_out[:, t, :], X[:, t, :])
                    dve.wait_ge(s1_used, (n + 1) * HG)
                    dve.tensor_scalar(per_head(qs, ni)[:, :, HEADS], mx[:], -1.0, None, ALU.mult).then_inc(m_ready, 1)
                if takes:
                    dve.wait_ge(pv_up, c + 1)
                    dve.wait_ge(y_up, c)
                    dve.tensor_copy(yc[:], psY[:]).then_inc(yc_ready, 1)

            norm(0)
            dve.wait_ge(*loaded["a"])
            dve.tensor_copy(K["ident_bf"][:], K["ident"][:]).then_inc(made, 1)
            dve.tensor_copy(K["masks_bf"][:], K["masks"][:]).then_inc(made, 1)
            step(-3, 1, False, False, False)
            dve.wait_ge(x_rest, 16 * (NT // PART - 1))
            stats(PART, NT)
            dve.memset(pad[:], 0.0)
            step(-2, 2, False, False)
            moments(dve, chained, st, mv, rstd, tmp, PART, NT + AHEAD, MOMENT_LINKS)
            step(-1, 3, False)
            with dve.Fori(0, BATCH) as b:
                for i in range(TILES):
                    step(b * TILES + i, i)

        @block.tensor
        def _(pe):
            pe.wait_ge(start, 7)
            pe.wait_ge(*loaded["a"])

            def masked(bank, mask):
                pe.matmul(bank[:], K["ident_bf"][:], mask.unsqueeze(1).broadcast_to([P, HG, P]), start=True, stop=True)

            def turn(n, t=None, c=None):
                pe.wait_ge(xn_ready, n + 1)
                if t is not None:
                    pe.wait_ge(x_done, t + 1)
                elif c is not None:
                    pe.wait_ge(q2_ready, c + 1)
                else:
                    pe.wait_ge(xT_ready, n)
                pe.transpose(psT[:, 0:P], xn[:], K["ident"][:]).then_inc(xT_up, 1)

            def step(t, i, ends=True, takes=True, scores=True):
                c, ci, n, ni, a, ai = t + 1, (i + 1) % TILES, t + 2, (i + 2) % TILES, t + 3, (i + 3) % TILES
                if scores:
                    pe.wait_ge(lo_ready, (n + 1) * 2)
                    pe.wait_ge(qkT_ready, n)
                    for g in range(HG):
                        pe.transpose(psD[:, g, :], qs[:, ni, g * P:(g + 1) * P], K["ident16"][:])
                        last = pe.transpose(psD[:, HG + g, :], ks[:, ni, g * P:(g + 1) * P], K["ident16"][:])
                    last.then_inc(st_up, 1)
                pe.wait_ge(xT_ready, a + 1)
                pe.wait_ge(rope_ready, a * 3)
                pe.wait_ge(v_ready, a)
                own = xnT[:, PAD + ai * P:PAD + (ai + 1) * P]
                pe.matmul(psA[:, 0:256], own, W["qkvT"][:, 0:256], start=True, stop=True)
                if takes:
                    pe.wait_ge(m_ready, c + 1)
                    for g in range(HG):
                        last = pe.transpose(psQ[:, g, :], qs[:, ci, g * P:(g + 1) * P], K["ident16"][:])
                    last.then_inc(q2_up, 1)
                pe.matmul(psA[:, 256:384], xnT[:, ai * P:(ai + 1) * P], W["qkvT"][:, 256:384], start=True, stop=True)
                pe.matmul(psA[:, 384:512], own, W["qkvT"][:, 256:384], start=True, stop=True).then_inc(qkv_up, 1)
                if ends:
                    pe.wait_ge(yc_ready, t + 1)
                    for r in range(HG):
                        last = pe.transpose(psY[:, r * P:(r + 1) * P], yc[:, r * P:(r + 1) * P], K["ident"][:])
                    last.then_inc(y_up, 1)

                def probabilities(r):
                    pe.wait_ge(q2_ready, c + 1)
                    pe.wait_ge(s1_used, c * HG + (r + 1))
                    masked(psS[r], K["mask_k"][:, 0 if ci == 0 else 1, :])
                    for g in range(HG):
                        for j in range(2):
                            w = 2 * ci + j
                            last = pe.matmul(psS[r][:, g * P + QB * j:g * P + QB * (j + 1)],
                                             qkT[ROWS * r:ROWS * r + HEADS + 1, HG + g, QB * w:QB * w + P],
                                             q2T[ROWS * r:ROWS * r + HEADS + 1, g, QB * j:QB * (j + 1)],
                                             start=False, stop=True, skip_group_check=True)
                    last.then_inc(s2_up, 1)

                def values(r):
                    pe.wait_ge(v_ready, c + 1)
                    pe.wait_ge(yn_ready, c)
                    pe.wait_ge(p_ready, c * HG + (r + 1))
                    for j in range(2):
                        for g in range(HG):
                            last = pe.matmul(psY[ROWS * g:ROWS * (g + 1), r * P + QB * j:r * P + QB * (j + 1)],
                                             v_sb[:, 2 * ci + j, HG * g + r, :],
                                             prob[:, r, g * P + QB * j:g * P + QB * (j + 1)], start=True, stop=True)
                    if r == HG - 1:
                        last.then_inc(pv_up, 1)

                def maxima(r):
                    pe.wait_ge(qkT_ready, n + 1)
                    if takes:
                        pe.wait_ge(p_ready, c * HG + (r + 1))
                    masked(psS[r], K["mask_q"][:, 0 if ni == 0 else 1, :])
                    for g in range(HG):
                        for j in range(2):
                            w = 2 * ni + j
                            last = pe.matmul(psS[r][QB * j:QB * (j + 1), g * P:(g + 1) * P],
                                             qkT[ROWS * r:ROWS * r + HEADS, g, PAD + QB * w:PAD + QB * (w + 1)],
                                             qkT[ROWS * r:ROWS * r + HEADS, HG + g, QB * w:QB * w + P],
                                             start=False, stop=True, skip_group_check=True)
                    last.then_inc(s1_up, 1)

                if takes:
                    probabilities(0)
                    probabilities(1)
                    if ends:
                        pe.wait_ge(yn_ready, t + 1)
                        pe.transpose(psT[:, 0:P], yn[:], K["ident"][:]).then_inc(yT_up, 1)
                for r in range(HG):
                    if takes and r < HG - 1:
                        values(r)
                    if scores:
                        maxima(r)
                    if r == 0 and ends:
                        pe.wait_ge(yT_ready, t + 1)
                        pe.matmul(psT[:, 0:C], yT[:], W["projT"][:], start=True, stop=True).then_inc(out_up, 1)
                    if takes and r < HG - 2:
                        probabilities(r + 2)
                if takes:
                    turn(a + 1, t if ends else None, c)
                    values(HG - 1)
                if not takes:
                    turn(a + 1)

            turn(0)
            step(-3, 1, False, False, False)
            pe.wait_ge(made, 2)
            step(-2, 2, False, False)
            step(-1, 3, False)
            with pe.Fori(0, BATCH) as b:
                for i in range(TILES):
                    step(b * TILES + i, i)


def mixture(nc, sb, psum, sem, X, K, W, tag, st, st_out=None, x_out=None):
    pad = sb(tag + "pad", [P, 1], F32)
    mv = sb(tag + "mv", [P, NT + TILES, 2], F32)
    rstd = sb(tag + "rstd", [P, NT + TILES, 1], F32)
    tmp = sb(tag + "tmp", [P, NT + TILES], F32)
    xn = sb(tag + "xn", [P, TILES, C], F32)
    xnT = sb(tag + "xnT", [P, T], F32)
    xh = sb(tag + "xh", [P, 2, T], F16)
    xl = sb(tag + "xl", [P, 2, T], F16)
    lg = sb(tag + "lg", [P, TILES, E], F32)
    top = sb(tag + "top", [P, TILES, 8], F32)
    idx = sb(tag + "idx", [P, TILES, 8], U32)
    idf = sb(tag + "idf", [P, TILES, 2], F32)
    gap = sb(tag + "gap", [P, TILES], F32)
    th = sb(tag + "th", [P, TILES], F32)
    w12 = sb(tag + "w12", [P, TILES, 2], F32)
    pick = sb(tag + "pick", [P, TILES, 2, E], F32)
    gate = sb(tag + "gate", [P, 2, TILES, E], F32)
    su = sb(tag + "su", [P, 2, T], F32)
    hf = sb(tag + "hf", [P, 2, T], F32)
    hh = sb(tag + "hh", [P, 4, T], F16)
    hl = sb(tag + "hl", [P, 4, T], F16)

    psU = [psum(f"{tag}psU{i}", [P, 512], F32) for i in range(2)]
    psV = [psum(f"{tag}psV{i}", [P, 512], F32) for i in range(2)]
    psY = [psum(f"{tag}psY{i}", [P, 512], F32) for i in range(2)]
    psT = psum(tag + "psT", [P, 512], F32)
    psL = psum(tag + "psL", [P, 512], F32)

    xn_ready = sem(tag + "xn_ready")
    xT_up = sem(tag + "xT_up")
    xT_ready = sem(tag + "xT_ready")
    xl_ready = sem(tag + "xl_ready")
    lg_up = sem(tag + "lg_up")
    gap_ready = sem(tag + "gap_ready")
    th_ready = sem(tag + "th_ready")
    u_up = sem(tag + "u_up")
    v_up = sem(tag + "v_up")
    su_ready = sem(tag + "su_ready")
    h_ready = sem(tag + "h_ready")
    hh_ready = sem(tag + "hh_ready")
    hl_ready = sem(tag + "hl_ready")
    y_up = sem(tag + "y_up")
    y_used = sem(tag + "y_used")
    dve_step = sem(tag + "dve_step")
    stored = sem(tag + "stored")
    FRONT = 9
    UNITS = E * HC
    NORM, TURN, LOGITS, GATES = 1, 2, 3, 6

    with nc.Block() as block:

        @block.vector
        def _(dve):
            dve.sem_inc(y_used, 2)

            def chained(ins, value):
                ins.then_inc(dve_step, 1)
                dve.wait_ge(dve_step, value)

            def norms(b):
                dve.wait_ge(xT_up, b)
                for i in range(TILES):
                    t = b * TILES + i
                    ins = dve.tensor_scalar(xn[:, i, :], X[:, t, :], mv[:, t, 0:1], rstd[:, t, :],
                                            ALU.subtract, ALU.mult)
                ins.then_inc(xn_ready, 1)

            def choose(b):
                s0 = b * FRONT + STAT_LINKS
                dve.wait_ge(lg_up, b + 1)
                chained(dve.tensor_copy(lg[:], psL[:, 0:TILES * E].rearrange("p (i e) -> p i e", e=E)), s0 + 1)
                dve.memset(pad[:], 0.0)
                for i in range(TILES):
                    ins = dve.max(top[:, i, :], lg[:, i, :])
                chained(ins, s0 + 2)
                dve.tensor_tensor(gap[:], top[:, :, 0], top[:, :, 1], ALU.subtract).then_inc(gap_ready, 1)
                for i in range(TILES):
                    ins = dve.max_index(idx[:, i, :], top[:, i, :], lg[:, i, :])
                chained(ins, s0 + 3)
                chained(dve.tensor_copy(idf[:], idx[:, :, 0:2]), s0 + 4)

            def gates(b, slot):
                s0 = b * FRONT + STAT_LINKS
                dve.wait_ge(th_ready, b + 1)
                half = 0.5 / Y_UP
                chained(dve.tensor_scalar(w12[:, :, 0], th[:], half, half, ALU.mult, ALU.add), s0 + 5)
                chained(dve.tensor_scalar(w12[:, :, 1], th[:], -half, half, ALU.mult, ALU.add), s0 + 6)
                every = [P, TILES, 2, E]
                chained(dve.tensor_tensor(pick[:], K["iota"][:].unsqueeze(1).unsqueeze(1).broadcast_to(every),
                                          idf[:].unsqueeze(3).broadcast_to(every), ALU.is_equal), s0 + 7)
                chained(dve.tensor_tensor(pick[:], pick[:], w12[:].unsqueeze(3).broadcast_to(every), ALU.mult), s0 + 8)
                chained(dve.tensor_tensor(gate[:, slot, :, :], pick[:, :, 0, :], pick[:, :, 1, :], ALU.add), s0 + 9)

            def hidden(b, n):
                dve.wait_ge(su_ready, b * UNITS + (n + 1))
                dve.wait_ge(v_up, b * UNITS + (n + 1))
                if n >= 2:
                    dve.wait_ge(hl_ready, b * UNITS + (n - 1))
                dve.tensor_tensor(hf[:, n % 2, :], su[:, n % 2, :], psV[n % 2][:], ALU.mult).then_inc(h_ready, 1)

            def collect(b, e, slot):
                dve.wait_ge(y_up, b * E + (e + 1))
                dve.wait_ge(y_used, b * E + (e + 2))
                for i in range(TILES):
                    ins = dve.scalar_tensor_tensor(X[:, b * TILES + i, :], psY[e % 2][:, i * P:(i + 1) * P],
                                                   gate[:, slot, i, e:e + 1], X[:, b * TILES + i, :],
                                                   ALU.mult, ALU.add)
                ins.then_inc(y_used, 1)

            dve.memset(mv[:, NT:, :], 1.0)
            moments(dve, chained, st, mv, rstd, tmp, 0, TILES, 0)
            norms(0)
            moments(dve, chained, st, mv, rstd, tmp, TILES, NT + TILES, MOMENT_LINKS)
            choose(0)
            gates(0, 0)
            for n in range(HC):
                hidden(0, n)
            with dve.Fori(0, BATCH // 2) as b2:
                for half in range(2):
                    b = b2 * 2 + half
                    for e in range(E):
                        for c in range(HC):
                            hidden(b, (e + 1) * HC + c)
                        collect(b, e, half)
                        if e == NORM - 1:
                            norms(b2 * 2 + (half + 1))
                        if e == LOGITS + 1:
                            choose(b2 * 2 + (half + 1))
                        if e == GATES:
                            gates(b2 * 2 + (half + 1), (half + 1) % 2)
                    if st_out is not None:
                        dve.wait_ge(y_used, b * E + (E + 2))
                        for i in range(TILES):
                            dve.bn_stats(st_out[:, b * TILES + i, :], X[:, b * TILES + i, :])

        @block.gpsimd
        def _(pool):
            def low_x(b, slot):
                pool.wait_ge(xT_ready, b * 2 + 2)
                pool.tensor_tensor(xl[:, slot, :], xnT[:], xh[:, slot, :], ALU.subtract).then_inc(xl_ready, 1)

            def low(b, n):
                pool.wait_ge(hh_ready, b * UNITS + (n + 1))
                pool.tensor_tensor(hl[:, n % 4, :], hf[:, n % 2, :], hh[:, n % 4, :], ALU.subtract).then_inc(hl_ready, 1)

            low_x(0, 0)
            for n in range(HC):
                low(0, n)
            with pool.Fori(0, BATCH // 2) as b2:
                for half in range(2):
                    for e in range(E):
                        for c in range(HC):
                            low(b2 * 2 + half, (e + 1) * HC + c)
                        if e == TURN:
                            low_x(b2 * 2 + (half + 1), (half + 1) % 2)

        @block.scalar
        def _(act):
            def turned(b, slot):
                act.wait_ge(xT_up, b + 1)
                act.wait_ge(xl_ready, b)
                act.copy(xnT[:], psT[:]).then_inc(xT_ready, 1)
                act.copy(xh[:, slot, :], psT[:]).then_inc(xT_ready, 1)

            def gap_tanh(b):
                act.wait_ge(gap_ready, b + 1)
                act.activation(th[:], gap[:], ACT.Tanh, scale=0.5).then_inc(th_ready, 1)

            def silu(b, n):
                act.wait_ge(u_up, b * UNITS + (n + 1))
                if n >= 2:
                    act.wait_ge(h_ready, b * UNITS + (n - 1))
                act.activation(su[:, n % 2, :], psU[n % 2][:], ACT.Silu, scale=1.0 / W_UP["w1"]).then_inc(su_ready, 1)

            def high(b, n):
                act.wait_ge(h_ready, b * UNITS + (n + 1))
                if n >= 4:
                    act.wait_ge(y_up, b * E + (n // HC - 1))
                elif n >= 2:
                    act.wait_ge(y_up, b * E)
                act.copy(hh[:, n % 4, :], hf[:, n % 2, :]).then_inc(hh_ready, 1)

            turned(0, 0)
            gap_tanh(0)
            for n in range(HC):
                silu(0, n)
                high(0, n)
            with act.Fori(0, BATCH // 2) as b2:
                for half in range(2):
                    b = b2 * 2 + half
                    for e in range(E):
                        for c in range(HC):
                            silu(b, (e + 1) * HC + c)
                        for c in range(HC):
                            high(b, (e + 1) * HC + c)
                        if e == TURN:
                            turned(b2 * 2 + (half + 1), (half + 1) % 2)
                        if e == LOGITS + 2:
                            gap_tanh(b2 * 2 + (half + 1))

        @block.tensor
        def _(pe):
            def turn(b):
                pe.wait_ge(xn_ready, b + 1)
                for i in range(TILES):
                    ins = pe.transpose(psT[:, i * P:(i + 1) * P], xn[:, i, :], K["ident"][:])
                ins.then_inc(xT_up, 1)

            def logits(b):
                pe.wait_ge(xT_ready, b * 2 + 1)
                for i in range(TILES):
                    ins = pe.matmul(psL[:, i * E:(i + 1) * E], xnT[:, i * P:(i + 1) * P], W["g"][:], start=True, stop=True)
                ins.then_inc(lg_up, 1)

            def thrice(out, wh, wl, slot):
                pe.matmul(out, wh, xh[:, slot, :], start=True, stop=False)
                pe.matmul(out, wh, xl[:, slot, :], start=False, stop=False)
                return pe.matmul(out, wl, xh[:, slot, :], start=False, stop=True)

            def up(b, e, slot):
                for c in range(HC):
                    n, ee, cols = e * HC + c, e % E, slice(c * P, (c + 1) * P)
                    if n >= 2:
                        pe.wait_ge(su_ready, b * UNITS + (n - 1))
                    thrice(psU[n % 2][:], W["w1h"][:, ee, cols], W["w1l"][:, ee, cols], slot).then_inc(u_up, 1)
                    if n >= 2:
                        pe.wait_ge(h_ready, b * UNITS + (n - 1))
                    thrice(psV[n % 2][:], W["w2h"][:, ee, cols], W["w2l"][:, ee, cols], slot).then_inc(v_up, 1)

            def down(b, e):
                pe.wait_ge(hl_ready, b * UNITS + (e + 1) * HC)
                pe.wait_ge(y_used, b * E + (e + 1))
                for i in range(TILES):
                    out = psY[e % 2][:, i * P:(i + 1) * P]
                    for c in range(HC):
                        s, tok = (e * HC + c) % 4, slice(i * P, (i + 1) * P)
                        pe.matmul(out, hh[:, s, tok], W["w3h"][:, e, c, :], start=(c == 0), stop=False)
                        pe.matmul(out, hh[:, s, tok], W["w3l"][:, e, c, :], start=False, stop=False)
                        ins = pe.matmul(out, hl[:, s, tok], W["w3h"][:, e, c, :], start=False, stop=(c == HC - 1))
                ins.then_inc(y_up, 1)

            turn(0)
            logits(0)
            pe.wait_ge(xl_ready, 1)
            up(0, 0, 0)
            with pe.Fori(0, BATCH // 2) as b2:
                for half in range(2):
                    b = b2 * 2 + half
                    for e in range(E):
                        if e == E - 1:
                            pe.wait_ge(xl_ready, b2 * 2 + (half + 2))
                        up(b, e + 1, half if e < E - 1 else (half + 1) % 2)
                        down(b, e)
                        if e == TURN - 1:
                            turn(b2 * 2 + (half + 1))
                        if e == LOGITS:
                            logits(b2 * 2 + (half + 1))

        if x_out is not None:
            @block.sync
            def _(sp):
                with sp.Fori(0, BATCH) as b:
                    sp.wait_ge(y_used, b * E + (E + 2))
                    sp.dma_start(x_out[:, bass.ds(b * TILES, TILES), :], X[:, bass.ds(b * TILES, TILES), :]).then_inc(stored, 16)
                sp.wait_ge(stored, 16 * BATCH)


def log_factors():
    roots = np.roots(LOG_POLY[::-1])
    real = [r.real for r in roots if abs(r.imag) < 1e-9]
    pairs = [(r.real, r.imag ** 2) for r in roots if r.imag > 1e-9]
    assert len(real) == 1 and len(pairs) == 2
    return float(LOG_POLY[-1]), float(real[0]), [(float(a), float(b)) for a, b in pairs]


def scan(nc, sb, psum, sem, X, K, W, loaded, st, st_out):
    mv = sb("s_mv", [P, NT, 2], F32)
    rstd = sb("s_rstd", [P, NT, 1], F32)
    tmp = sb("s_tmp", [P, NT], F32)
    xn = sb("s_xn", [P, TILES, C], F32)
    xnT = sb("s_xnT", [P, 2, T], F32)
    rT = sb("s_rT", [RANK, T], F32)
    ez = sb("s_ez", [P, T], F32)
    sq = sb("s_sq", [P, 2, T], F32)
    lp = sb("s_lp", [P, T], F32)
    dlt = sb("s_dlt", [P, T], F32)
    dx = sb("s_dx", [P, T], F32)
    halves = sb("s_halves", [P, 4, T], F16)
    spreads = sb("s_spreads", [P, 2, QUARTERS, T], F16)
    Brep = sb("s_Brep", [P, 2, T], F32)
    Crep = sb("s_Crep", [P, 2, T], F32)
    abar = sb("s_abar", [P, 4, T], F32)
    dbx = sb("s_dbx", [P, 4, T], F32)
    hst = sb("s_hst", [P, 4, T], F32)
    hc = sb("s_hc", [P, 8, T], F32)
    yT = sb("s_yT", [P, T], F32)
    lead, root, pairs = log_factors()
    D_diag = sb("s_D_diag", [P, P], F32)
    shift = sb("s_shift", [P, 3], F32)

    psE = [psum(f"s_psE{i}", [P, 512], F32) for i in range(2)]
    psX = [psum(f"s_psX{i}", [P, 512], F32) for i in range(4)]
    psY = psum("s_psY", [P, 512], F32)
    psT = psum("s_psT", [P, 512], F32)

    A_ready = sem("s_A_ready")
    made = sem("s_made")
    xn_ready = sem("s_xn_ready")
    xT_up = sem("s_xT_up")
    xT_ready = sem("s_xT_ready")
    proj_up = sem("s_proj_up")
    proj_used = sem("s_proj_used")
    sq_ready = sem("s_sq_ready")
    hi_ready = sem("s_hi_ready")
    lo_ready = sem("s_lo_ready")
    spreads_ready = sem("s_spreads_ready")
    e_up = sem("s_e_up")
    x_up = sem("s_x_up")
    a_ready = sem("s_a_ready")
    dbx_ready = sem("s_dbx_ready")
    h_ready = sem("s_h_ready")
    hc_ready = sem("s_hc_ready")
    gathered = sem("s_gathered")
    y_ready = sem("s_y_ready")
    o_up = sem("s_o_up")
    x_done = sem("s_x_done")
    dve_step = sem("s_dve_step")
    LINKS = 6
    MOVES = 16 * 4 * QUARTERS
    LAG = 6
    Y, OUT, ADD = G + LAG, G + LAG + 1, G + LAG + 1
    BODY = {"norm": 8, "turn": 12, "r": 13, "z": 14, "squares": 14, "deltas": (14, 15, 16, 17, 19), "high": 17, "B": 19, "C": 20}
    HEAD = {"norm": 0, "turn": 1, "r": 2, "z": 3, "squares": 3, "deltas": (3, 4, 5, 6, 7), "high": 6, "B": 4, "C": 5}
    FIRST = ADD + 1 - G
    assert FIRST == BODY["norm"] and FIRST > HEAD["deltas"][-1]

    def turns(eng, steps):
        steps(0, 0, 0, FIRST, 1, HEAD)
        with eng.Fori(0, BATCH // 2 - 1) as b2:
            for half in range(2):
                steps(b2 * 2 + half, half, FIRST, G + FIRST, b2 * 2 + (half + 2), BODY)
        steps(BATCH - 2, 0, FIRST, G + FIRST, None, {})
        steps(BATCH - 1, 1, FIRST, G + FIRST, None, {})

    def has(b, g):
        return not isinstance(b, int) or b * G + g < BATCH * G

    with nc.Block() as block:

        @block.vector
        def _(dve):
            dve.memset(shift[:, 0:1], -pairs[0][0])
            dve.memset(shift[:, 1:2], -pairs[1][0])
            dve.memset(shift[:, 2:3], pairs[1][1])
            dve.wait_ge(*loaded["s"])
            dve.tensor_scalar(D_diag[:], K["ident"][:], W["D"][:], None, ALU.mult).then_inc(made, 1)

            def chained(ins, value):
                ins.then_inc(dve_step, 1)
                dve.wait_ge(dve_step, value)

            def norms(b):
                dve.wait_ge(xT_up, b)
                for i in range(TILES):
                    t = b * TILES + i
                    ins = dve.tensor_scalar(xn[:, i, :], X[:, t, :], mv[:, t, 0:1], rstd[:, t, :],
                                            ALU.subtract, ALU.mult)
                ins.then_inc(xn_ready, 1)

            def deltas(b, slot, k):
                at = STAT_LINKS + b * LINKS
                if k == 0:
                    dve.wait_ge(proj_used, b * 4 + 2)
                    chained(dve.tensor_scalar(ez[:], ez[:], E_MAX, None, ALU.min), at + 1)
                elif k == 1:
                    dve.wait_ge(sq_ready, b * 2 + 2)
                    chained(dve.scalar_tensor_tensor(lp[:], sq[:, 0, :], pairs[0][1], sq[:, 1, :], ALU.add, ALU.mult), at + 2)
                    chained(dve.scalar_tensor_tensor(lp[:], ez[:], -root, lp[:], ALU.add, ALU.mult), at + 3)
                elif k == 2:
                    chained(dve.scalar_tensor_tensor(lp[:], lp[:], lead, ez[:], ALU.mult, ALU.mult), at + 4)
                    chained(dve.tensor_scalar(dlt[:], lp[:], DT_MIN, DT_MAX, ALU.max, ALU.min), at + 5)
                elif k == 3:
                    dve.wait_ge(xT_ready, b + 1)
                    chained(dve.tensor_tensor(dx[:], dlt[:], xnT[:, slot, :], ALU.mult), at + 6)
                elif k == 4:
                    dve.wait_ge(hi_ready, b * 2 + 2)
                    dve.wait_ge(spreads_ready, b * MOVES)
                    for n, whole in enumerate((dlt, dx)):
                        dve.scalar_tensor_tensor(halves[:, 2 * n + 1, :], whole[:], UP, halves[:, 2 * n, :],
                                                 ALU.mult, ALU.subtract).then_inc(lo_ready, 1)

            def drive(b, g, slot):
                dve.wait_ge(x_up, b * G + (g + 1))
                if g % G == 0:
                    dve.wait_ge(proj_used, b * 4 + (g // G * 4 + 3))
                if g >= 4:
                    dve.wait_ge(h_ready, b * G + (g - 3))
                dve.tensor_tensor(dbx[:, g % 4, :], psX[g % 4][:], Brep[:, slot, :], ALU.mult).then_inc(dbx_ready, 1)

            def states(b, g):
                dve.wait_ge(a_ready, b * G + (g + 1))
                dve.wait_ge(dbx_ready, b * G + (g + 1))
                if g >= 4:
                    dve.wait_ge(hc_ready, b * G + (g - 3))
                dve.tensor_tensor_scan(hst[:, g % 4, :], abar[:, g % 4, :], dbx[:, g % 4, :], 0.0,
                                       ALU.mult, ALU.add).then_inc(h_ready, 1)

            def steps(b, half, first, end, n, at):
                for g in range(first, end):
                    if has(b, g):
                        drive(b, g, (half + g // G) % 2)
                    if g >= 1 and has(b, g - 1):
                        states(b, g - 1)
                    if g == at.get("norm"):
                        norms(n)
                    if g in at.get("deltas", ()):
                        deltas(n, (half if first else 1), at["deltas"].index(g))
                    if g == ADD:
                        dve.wait_ge(o_up, b + 1)
                        rows = X[:, bass.ds(b * TILES, TILES), :]
                        dve.tensor_tensor(rows, rows, psT[:].rearrange("p (i c) -> p i c", c=C), ALU.add).then_inc(x_done, 1)
                        dve.wait_ge(x_done, b + 1)
                        for i in range(TILES):
                            dve.bn_stats(st_out[:, b * TILES + i, :], X[:, b * TILES + i, :])

            moments(dve, chained, st, mv, rstd, tmp, 0, TILES, 0)
            norms(0)
            dve.wait_ge(A_ready, 1)
            dve.tensor_scalar(W["A"][:], W["A"][:], -1.0 / UP, None, ALU.mult).then_inc(A_ready, 1)
            moments(dve, chained, st, mv, rstd, tmp, TILES, NT, MOMENT_LINKS)
            for k in range(5):
                deltas(0, 0, k)
            turns(dve, steps)

        @block.gpsimd
        def _(pool):
            def steps(b, half, first, end, n, at):
                for g in range(first, end):
                    if not has(b, g):
                        break
                    pool.wait_ge(h_ready, b * G + (g + 1))
                    if g % G == 0:
                        pool.wait_ge(proj_used, b * 4 + (g // G * 4 + 4))
                    if g >= 8:
                        pool.wait_ge(gathered, b * SUBS + (g // QUARTERS - 1))
                    pool.tensor_tensor(hc[:, g % 8, :], hst[:, g % 4, :], Crep[:, (half + g // G) % 2, :],
                                       ALU.mult).then_inc(hc_ready, 1)

            turns(pool, steps)

        @block.sync
        def _(sp):
            def move(b, slot):
                for n, ready, count in ((0, hi_ready, 1), (2, hi_ready, 2), (1, lo_ready, 1), (3, lo_ready, 2)):
                    sp.wait_ge(ready, b * 2 + count)
                    for q in range(QUARTERS):
                        sp.dma_start(spreads[QUARTER * n:QUARTER * (n + 1), slot, q, :],
                                     halves[QUARTER * q:QUARTER * (q + 1), n, :]).then_inc(spreads_ready, 16)

            move(0, 0)
            with sp.Fori(0, BATCH // 2 - 1) as b2:
                for half in range(2):
                    move(b2 * 2 + (half + 1), (half + 1) % 2)
            move(BATCH - 1, 1)
            sp.wait_ge(spreads_ready, BATCH * MOVES)

        @block.scalar
        def _(act):
            act.wait_ge(*loaded["s"])
            act.activation(W["A"][:], W["A"][:], ACT.Exp).then_inc(A_ready, 1)

            def turned(b, slot):
                act.wait_ge(xT_up, b + 1)
                act.copy(xnT[:, slot, :], psT[:]).then_inc(xT_ready, 1)

            def projected(b, slot, k):
                act.wait_ge(proj_up, b * 4 + (k + 1))
                if k == 0:
                    ins = act.copy(rT[:], psT[0:RANK, :])
                elif k == 1:
                    act.wait_ge(lo_ready, b * 2)
                    ins = act.activation(ez[:], psT[:], ACT.Exp, bias=W["dtb"][:])
                elif k == 2:
                    ins = act.mul(Brep[:, slot, :], psT[:], 1.0 / UP)
                else:
                    ins = act.copy(Crep[:, slot, :], psT[:])
                ins.then_inc(proj_used, 1)

            def squares(b):
                act.wait_ge(dve_step, STAT_LINKS + b * LINKS + 1)
                act.wait_ge(made, 1)
                act.activation(sq[:, 0, :], ez[:], ACT.Square, bias=shift[:, 0:1])
                act.activation(sq[:, 1, :], ez[:], ACT.Square, bias=shift[:, 1:2]).then_inc(sq_ready, 1)
                act.wait_ge(sq_ready, b * 2 + 1)
                act.activation(sq[:, 1, :], sq[:, 1, :], ACT.Identity, bias=shift[:, 2:3]).then_inc(sq_ready, 1)

            def high(b):
                for n, whole in enumerate((dlt, dx)):
                    act.wait_ge(dve_step, STAT_LINKS + b * LINKS + 5 + n)
                    act.wait_ge(spreads_ready, b * MOVES)
                    act.mul(halves[:, 2 * n, :], whole[:], UP).then_inc(hi_ready, 1)

            def steps(b, half, first, end, n, at):
                slot = (half if first else 1)
                for g in range(first, end):
                    if has(b, g):
                        act.wait_ge(e_up, b * G + (g + 1))
                        if g >= 4:
                            act.wait_ge(h_ready, b * G + (g - 3))
                        act.activation(abar[:, g % 4, :], psE[g % 2][:], ACT.Exp, scale=W["A"][:, g % G:g % G + 1]).then_inc(a_ready, 1)
                    if g == at.get("turn"):
                        if first:
                            act.wait_ge(gathered, b * SUBS + 1)
                        turned(n, slot)
                    for k, part in enumerate(("r", "z", "B", "C")):
                        if g == at.get(part):
                            if first and part == "C":
                                act.wait_ge(hc_ready, b * G + G)
                            projected(n, slot, k)
                    if g == at.get("squares"):
                        squares(n)
                    if g == at.get("high"):
                        high(n)
                    if g == Y:
                        act.wait_ge(gathered, b * SUBS + SUBS)
                        act.copy(yT[:], psY[:]).then_inc(y_ready, 1)

            turned(0, 0)
            for k in range(4):
                projected(0, 0, k)
                if k == 1:
                    squares(0)
            high(0)
            act.wait_ge(A_ready, 2)
            turns(act, steps)

        @block.tensor
        def _(pe):
            pe.wait_ge(*loaded["s"])
            pe.wait_ge(made, 1)

            def turn(b, o=None):
                pe.wait_ge(xn_ready, b + 1)
                if o is not None:
                    pe.wait_ge(x_done, o)
                else:
                    pe.wait_ge(proj_used, b * 4)
                for i in range(TILES):
                    ins = pe.transpose(psT[:, i * P:(i + 1) * P], xn[:, i, :], K["ident"][:])
                ins.then_inc(xT_up, 1)

            def project(b, slot, k):
                if k == 0:
                    pe.wait_ge(xT_ready, b + 1)
                pe.wait_ge(proj_used, b * 4 + k)
                if k == 0:
                    ins = pe.matmul(psT[0:RANK, :], W["xpT"][:], xnT[:, slot, :], start=True, stop=True)
                elif k == 1:
                    ins = pe.matmul(psT[:], W["dtT"][:], rT[:], start=True, stop=True)
                else:
                    ins = pe.matmul(psT[:], W["BT" if k == 2 else "CT"][:], xnT[:, slot, :], start=True, stop=True)
                ins.then_inc(proj_up, 1)

            def spread(b, g, slot):
                q, sub = g % QUARTERS, g % G // QUARTERS
                if g % G == 0:
                    pe.wait_ge(spreads_ready, (b + (g // G + 1)) * MOVES)
                if g >= 2:
                    pe.wait_ge(a_ready, b * G + (g - 1))
                if g >= 4:
                    pe.wait_ge(dbx_ready, b * G + (g - 3))
                for rows, bank, up in ((slice(0, P // 2), psE[g % 2], e_up), (slice(P // 2, P), psX[g % 4], x_up)):
                    pe.matmul(bank[:], K["sel"][rows, sub * P:(sub + 1) * P], spreads[rows, slot, q, :],
                              start=True, stop=True).then_inc(up, 1)

            def gather(b, g, slot):
                pe.wait_ge(hc_ready, b * G + (g + QUARTERS))
                if g % G == 0:
                    pe.wait_ge(y_ready, b + g // G)
                    pe.matmul(psY[:], D_diag[:], xnT[:, slot, :], start=True, stop=True)
                for k in range(g, g + QUARTERS):
                    q, sub = k % QUARTERS, k % G // QUARTERS
                    ins = pe.matmul(psY[QUARTER * q:QUARTER * (q + 1), :], K["selT"][:, sub * QUARTER:(sub + 1) * QUARTER],
                                    hc[:, k % 8, :], start=False, stop=True, skip_group_check=True)
                ins.then_inc(gathered, 1)

            def steps(b, half, first, end, n, at):
                for g in range(first, end):
                    if has(b, g):
                        spread(b, g, (half + g // G) % 2)
                    k = g - LAG
                    if k >= 0 and k % QUARTERS == QUARTERS - 1 and has(b, k):
                        gather(b, k - (QUARTERS - 1), (half + k // G) % 2)
                    if g == at.get("turn"):
                        turn(n, b if first else None)
                    for k, part in enumerate(("r", "z", "B", "C")):
                        if g == at.get(part):
                            project(n, (half if first else 1), k)
                    if g == OUT:
                        pe.wait_ge(y_ready, b + 1)
                        if n is not None:
                            pe.wait_ge(proj_used, (b + 3) * 4)
                        for i in range(TILES):
                            ins = pe.transpose(psT[:, i * P:(i + 1) * P], yT[:, i * P:(i + 1) * P], K["ident"][:])
                        ins.then_inc(o_up, 1)

            turn(0)
            for k in range(4):
                project(0, 0, k)
            turns(pe, steps)


def build(nc, x_in, x_out, dram, phases=4):
    with ExitStack() as outer:
        def keep(name, shape, dt):
            return outer.enter_context(nc.sbuf_tensor(name, shape, dt))

        def sem(name):
            return outer.enter_context(nc.semaphore(name))

        X = keep("X", [P, NT + TILES, C], F32)
        K = {n: keep("k_" + n, list(s), dt) for n, s, dt in (
            ("ident", (P, P), F32), ("ident16", (P, P), F16), ("masks", (P, 2, 2, P), F32),
            ("cos", (P, TILES, 4), F32), ("sin", (P, TILES, 4), F32), ("nsin", (P, TILES, 4), F32),
            ("iota", (P, E), F32), ("sel", (P, SUBS * P), F16), ("selT", (P, SUBS * QUARTER), F32))}
        ident_bf = keep("ident_bf", [P, P], BF16)
        masks_bf = keep("masks_bf", [P, 2, 2, P], BF16)
        W = {n: keep("w_" + n, list(s), F32) for n, s in (
            ("qkvT", (P, 3 * C)), ("projT", (P, C)), ("g", (P, E)), ("w1", (P, E, HID)), ("w2", (P, E, HID)),
            ("w3", (P, E, HC, C)), ("A", (P, G)), ("D", (P, 1)), ("dtb", (P, 1)), ("xpT", (P, RANK)),
            ("dtT", (RANK, P)), ("BT", (P, P)), ("CT", (P, P)))}
        for n, s in (("w1", (P, E, HID)), ("w2", (P, E, HID)), ("w3", (P, E, HC, C))):
            for half in "hl":
                W[n + half] = keep("w_" + n + half, list(s), F16)

        groups = {
            "a": ("ident", "masks", "ident16", "qkvT", "cos", "sin", "nsin", "projT"),
            "w": ("w1", "w2", "w3", "g", "iota"),
            "s": ("A", "D", "dtb", "xpT", "dtT", "BT", "CT", "sel", "selT"),
        }
        loaded = {g: (sem("loaded_" + g), 16 * len(names)) for g, names in groups.items()}
        st = [keep(f"st{k}", [P, NT, 6], F32) for k in range(2)]
        K["ident_bf"] = ident_bf
        K["masks_bf"], K["mask_q"], K["mask_k"] = masks_bf, masks_bf[:, 0], masks_bf[:, 1]

        def stage(n, fn, *args):
            if phases < n:
                return
            with ExitStack() as ctx:
                def sb(name, shape, dt):
                    return ctx.enter_context(nc.sbuf_tensor(name, shape, dt))

                def psum(name, shape, dt):
                    return ctx.enter_context(nc.psum_tensor(name, shape, dt))
                fn(nc, sb, psum, sem, X, K, W, *args)

        xo = x_out.rearrange("(t p) c -> p t c", p=P)
        stage(1, attention, x_in, dram, groups, loaded, st[0])
        stage(2, mixture, "f_", st[0], st[1])
        stage(3, scan, loaded, st[1], st[0])
        stage(4, mixture, "g_", st[0], None, xo)
        if phases < 4:
            stored = sem("stored")
            with nc.Block() as block:
                @block.sync
                def _(sp):
                    sp.dma_start(xo, X[:, 0:NT, :]).then_inc(stored, 16)
                    sp.wait_ge(stored, 16)


def constants():
    f = np.float32
    inv = (1.0 / np.float32(10000.0) ** (np.arange(0, D, 2, dtype=f) / f(D))).astype(f)
    ang = np.outer(np.arange(T, dtype=f), inv).astype(f).reshape(TILES, P, 4).transpose(1, 0, 2)
    p = np.arange(P)[:, None]
    k = np.arange(P)[None, :]
    q = p % QB
    ok = (k >= q) & (k <= q + QB)
    ok0 = ok & ((k >= QB) | (p >= QB))
    mask_q = np.stack([ok0, ok], 1)
    kk, col = p, k
    okk = (kk >= col % QB) & (kk <= col % QB + QB)
    okk0 = okk & ((kk >= QB) | (col >= QB))
    mask_k = np.stack([okk0, okk], 1)
    NEG = -1e30
    sel = (p[:, :, None] % QUARTER == DG * np.arange(SUBS)[None, :, None] + k[:, None, :] // NS)
    sel_t = (np.arange(QUARTER)[None, None, :] == DG * np.arange(SUBS)[None, :, None] + p[:, :, None] // NS)
    return {
        "ident": np.eye(P, dtype=f), "ident16": np.eye(P, dtype=np.float16),
        "masks": np.stack([np.where(m, 0, NEG) for m in (mask_q, mask_k)], 1).astype(f),
        "cos": np.cos(ang).astype(f), "sin": np.sin(ang).astype(f), "nsin": (-np.sin(ang)).astype(f),
        "iota": np.tile(np.arange(E, dtype=f), (P, 1)),
        "sel": sel.reshape(P, SUBS * P).astype(np.float16), "selT": sel_t.reshape(P, SUBS * QUARTER).astype(f),
    }


PHASES = 4


def kernel(**inputs):
    import concourse.bacc as bacc
    from concourse.bass_utils import run_bass_kernel_spmd

    a = {n: np.asarray(v) for n, v in inputs.items()}
    lay = {
        "x": a["L0_attn_a_x"].reshape(BATCH * T, C),
        "qkvT": a["L0_attn_a_w_attn"].T, "projT": a["L0_attn_a_w_proj"].T,
        "g": a["L0_ffn_Wg"],
        "w1": a["L0_ffn_W1"].transpose(1, 0, 2), "w2": a["L0_ffn_W2"].transpose(1, 0, 2),
        "w3": a["L0_ffn_W3"].reshape(E, HC, P, C).transpose(2, 0, 1, 3),
        "A": a["L0_attn_b_A_log"].reshape(QUARTERS, SUBS, DG * NS).transpose(2, 1, 0).reshape(P, G),
        "D": a["L0_attn_b_D"].reshape(P, 1), "dtb": a["L0_attn_b_dt_proj_b"].reshape(P, 1),
        "xpT": a["L0_attn_b_x_proj_w"].T, "dtT": a["L0_attn_b_dt_proj_w"].T,
        "BT": np.tile(a["L0_attn_b_B_proj_w"].T, (1, DG)), "CT": np.tile(a["L0_attn_b_C_proj_w"].T, (1, DG)),
    }
    lay.update(constants())
    arrays = {n + "_dram": np.ascontiguousarray(v) for n, v in lay.items()}
    nc = bacc.Bacc("TRN2", target_bir_lowering=False, num_devices=1)
    dram = {n[:-5]: nc.dram_tensor(n, v.shape, mybir.dt.from_np(v.dtype), kind="ExternalInput").ap() for n, v in arrays.items()}
    out = nc.dram_tensor("out_dram", (BATCH * T, C), F32, kind="ExternalOutput").ap()
    build(nc, dram["x"], out, dram, PHASES)
    r = run_bass_kernel_spmd(nc, [arrays], core_ids=[0])
    return r.results[0]["out_dram"].reshape(BATCH, T, C)
```

```python
from contextlib import ExitStack

import numpy as np

import concourse.bass as bass
from concourse import mybir

ALU = mybir.AluOpType
ACT = mybir.ActivationFunctionType
AX_X = mybir.AxisListType.X
F32 = mybir.dt.float32
F16 = mybir.dt.float16
BF16 = mybir.dt.bfloat16
U32 = mybir.dt.uint32
I32 = mybir.dt.int32

P = 128
BATCH, T, C = 8, 512, 128
TILES = T // P
NT = BATCH * TILES
H, D = 16, 8
WINDOW = 64
QB = WINDOW
HG = 4
ROWS = 32
E, HID = 8, 256
HC = HID // P
NS = 16
DG = P // NS
G = C // DG
QUARTER, QUARTERS = 32, C // 32
SUBS = G // QUARTERS
RANK = 64
EPS = 1e-5
DT_MIN, DT_MAX = 0.001, 0.1
UP = 1024.0
W_UP = {"w1": 16.0, "w2": 8.0, "w3": 16.0}
Y_UP = W_UP["w2"] * W_UP["w3"]
E_MAX = 0.1052
LOG_POLY = np.polynomial.chebyshev.Chebyshev.interpolate(
    lambda e: np.log1p(e) / e, 5, domain=[1e-9, E_MAX]).convert(kind=np.polynomial.Polynomial).coef


RSQRT_LINKS = 12
MOMENT_LINKS = 1 + RSQRT_LINKS
STAT_LINKS = 2 * MOMENT_LINKS


def rsqrt(dve, chained, v, y, t, first):
    chained(dve.tensor_scalar(v, v, EPS, None, ALU.add), first + 1)
    chained(dve.tensor_scalar(t.bitcast(I32), v.bitcast(I32), 1, None, ALU.logical_shift_right), first + 2)
    dve.tensor_scalar(y.bitcast(I32), t.bitcast(I32), -1.0, float(0x5F3759DF), ALU.mult, ALU.add)
    chained(dve.tensor_scalar(v, v, -0.5, None, ALU.mult), first + 3)
    for k in range(3):
        chained(dve.tensor_tensor(t, y, y, ALU.mult), first + 4 + 3 * k)
        chained(dve.tensor_tensor(t, t, v, ALU.mult), first + 5 + 3 * k)
        chained(dve.scalar_tensor_tensor(y, t, 1.5, y, ALU.add, ALU.mult), first + 6 + 3 * k)


def moments(dve, chained, st, mv, rstd, tmp, t0, end, link):
    for t in range(t0, end):
        ins = dve.bn_aggr(mv[:, t, :], st[:, t, :])
    chained(ins, link + 1)
    rsqrt(dve, chained, mv[:, t0:end, 1], rstd[:, t0:end, 0], tmp[:, t0:end], link + 1)


def attention(nc, sb, psum, sem, X, K, W, x_in, dram, groups, loaded, st_out):
    assert E == BATCH
    PAD = QB
    PART = NT // 8
    st = sb("a_st", [P, NT, 6], F32)
    mv = sb("a_mv", [P, NT, 2], F32)
    rstd = sb("a_rstd", [P, NT, 1], F32)
    tmp = sb("a_tmp", [P, NT], F32)
    pad = sb("a_pad", [P, 1], F32)
    xn = sb("a_xn", [P, C], F32)
    xnT = sb("a_xnT", [P, PAD + T], F32)
    rot_cos = sb("a_rot_cos", [P, 2 * C], F32)
    rot_sin = sb("a_rot_sin", [P, 2 * C], F32)
    rot = sb("a_rot", [P, 2 * C], F32)
    qs = sb("a_qs", [P, TILES, H * ROWS], F16)
    ks = sb("a_ks", [P, TILES, H * ROWS], F16)
    qkT = sb("a_qkT", [P, 2 * HG, PAD + T], F16)
    q2T = sb("a_q2T", [P, HG, P], F16)
    v_sb = sb("a_v", [P, 2 * TILES, H, ROWS], F32)
    mx = sb("a_mx", [P, H], F32)
    prob = sb("a_prob", [P, HG, HG * P], F32)
    yc = sb("a_yc", [P, HG * P], F32)
    rden = sb("a_rden", [P, H], F32)
    yn = sb("a_yn", [P, C], F32)
    yT = sb("a_yT", [P, C], F32)

    psS = [psum(f"a_psS{r}", [P, 512], F32) for r in range(HG)]
    psA = psum("a_psA", [P, 512], F32)
    psD = psum("a_psD", [P, 2 * HG, P], F16)
    psT = psum("a_psT", [P, 512], F32)
    psY = psum("a_psY", [P, 512], F32)

    psQ = psT[:, 0:HG * P // 2].bitcast(F16).rearrange("p (g q) -> p g q", g=HG)

    x_first = sem("a_x_first")
    x_rest = sem("a_x_rest")
    made = sem("a_made")
    stats_ready = sem("a_stats_ready")
    start = sem("a_start")
    xn_ready = sem("a_xn_ready")
    xT_up = sem("a_xT_up")
    xT_ready = sem("a_xT_ready")
    qkv_up = sem("a_qkv_up")
    v_ready = sem("a_v_ready")
    rope_ready = sem("a_rope_ready")
    rot_ready = sem("a_rot_ready")
    hi_ready = sem("a_hi_ready")
    lo_ready = sem("a_lo_ready")
    st_up = sem("a_st_up")
    qkT_ready = sem("a_qkT_ready")
    s1_up = sem("a_s1_up")
    s1_used = sem("a_s1_used")
    m_ready = sem("a_m_ready")
    q2_up = sem("a_q2_up")
    q2_ready = sem("a_q2_ready")
    s2_up = sem("a_s2_up")
    p_ready = sem("a_p_ready")
    pv_up = sem("a_pv_up")
    yc_ready = sem("a_yc_ready")
    y_up = sem("a_y_up")
    rden_ready = sem("a_rden_ready")
    yn_ready = sem("a_yn_ready")
    yT_up = sem("a_yT_up")
    yT_ready = sem("a_yT_ready")
    out_up = sem("a_out_up")
    x_done = sem("a_x_done")
    w_high = sem("a_w_high")
    w_low = sem("a_w_low")
    dve_step = sem("a_dve_step")
    HEADS = 24

    def stages(t):
        return tuple(not isinstance(t, int) or 0 <= t + k < NT for k in range(3))

    def exists(t):
        return not isinstance(t, int) or t < NT

    def per_head(stack, slot):
        return stack[:, slot, :].rearrange("p (h r) -> p h r", r=ROWS)

    with nc.Block() as block:

        @block.sync
        def _(sp):
            xin = x_in.rearrange("(t p) c -> p t c", p=P)

            def load(group):
                for n in groups[group]:
                    sp.dma_start((K[n] if n in K else W[n])[:], dram[n]).then_inc(loaded[group][0], 16)

            for t in range(0, NT, PART):
                sp.dma_start(X[:, t:t + PART, :], xin[:, t:t + PART, :]).then_inc(x_first if t == 0 else x_rest, 16)
                if t == 0:
                    load("a")
            load("w")
            load("s")

        @block.gpsimd
        def _(pool):
            pool.memset(xnT[:, 0:PAD], 0.0).then_inc(start, 1)
            pool.memset(qkT[:, :, 0:PAD], 0.0).then_inc(start, 1)
            pool.memset(v_sb[:], 0.0).then_inc(start, 1)
            pool.wait_ge(start, 5)
            pool.memset(v_sb[:, :, :, D:D + 1], 1.0).then_inc(start, 1)
            pool.memset(ks[:].rearrange("p s (h r) -> p (s h) r", r=ROWS)[:, :, HEADS:HEADS + 1], 1.0).then_inc(start, 1)

            def stack(n, i):
                pool.wait_ge(rope_ready, (n + 1) * 3)
                pool.wait_ge(lo_ready, n * 2)
                pool.tensor_tensor(rot[:], rot_cos[:], rot_sin[:], ALU.add).then_inc(rot_ready, 1)
                for half, out in ((0, per_head(qs, i)), (1, per_head(ks, i)[:, :, 0:16])):
                    cos, sin = (x[:, half * C:(half + 1) * C].rearrange("p (h d) -> p h d", d=D).unsqueeze(2)
                                .broadcast_to([P, H, 2, D]) for x in (rot_cos, rot_sin))
                    pool.tensor_tensor(out.rearrange("p h (a d) -> p h a d", a=2)[:, :, :, 0:D], cos, sin,
                                       ALU.add).then_inc(hi_ready, 1)
                pool.wait_ge(rot_ready, n + 1)
                pool.wait_ge(hi_ready, (n + 1) * 2)
                for half, out, lo in ((0, per_head(qs, i), 8), (1, per_head(ks, i), 16)):
                    pool.tensor_tensor(out[:, :, lo:lo + 8], rot[:, half * C:(half + 1) * C].rearrange("p (h d) -> p h d", d=D),
                                       out[:, :, 0:8], ALU.subtract).then_inc(lo_ready, 1)

            def low_weights(e, k, n):
                pool.wait_ge(w_high, e * 3 + (k + 1))
                w, h, lo = (x[:, e].rearrange("p a c -> p (a c)") if n == "w3" else x[:, e, :]
                            for x in (W[n], W[n + "h"], W[n + "l"]))
                pool.tensor_tensor(lo, w, h, ALU.subtract).then_inc(w_low, 1)

            for n in range(3):
                stack(n, n)

            def row(b):
                for i in range(TILES):
                    if exists(b * TILES + (i + 3)):
                        stack(b * TILES + (i + 3), (i + 3) % TILES)
                    if i > 0:
                        low_weights(b, i - 1, ("w1", "w2", "w3")[i - 1])

            with pool.Fori(0, BATCH - 1) as b:
                row(b)
            row(BATCH - 1)
            pool.wait_ge(w_low, 3 * E)

        @block.scalar
        def _(act):
            act.wait_ge(start, 7)

            def turned(n, ni):
                act.wait_ge(xT_up, n + 1)
                act.copy(xnT[:, PAD + ni * P:PAD + (ni + 1) * P], psT[:, 0:P]).then_inc(xT_ready, 1)

            def step(t, i, weights=()):
                c, n, ni, a, ai = t + 1, t + 2, (i + 2) % TILES, t + 3, (i + 3) % TILES
                ends, takes, scores = stages(t)

                def exponentials(r):
                    if takes:
                        act.wait_ge(pv_up, c)
                        act.wait_ge(s2_up, c * HG + (r + 1))
                        act.activation(prob[:, r, :], psS[r][:], ACT.Exp, scale=float(D) ** -0.5).then_inc(p_ready, 1)

                if scores:
                    act.wait_ge(st_up, n + 1)
                    act.copy(qkT[:, :, PAD + ni * P:PAD + (ni + 1) * P], psD[:]).then_inc(qkT_ready, 1)
                if weights:
                    high_weights(*weights)
                exponentials(0)
                if ends:
                    act.wait_ge(yT_up, t + 1)
                    act.copy(yT[:], psT[:, 0:P]).then_inc(yT_ready, 1)
                exponentials(1)
                if exists(a):
                    act.wait_ge(rope_ready, (a + 1) * 3)
                    act.copy(v_sb[:, 2 * ai:2 * ai + 2, :, 0:D],
                             psA[:, 256:512].rearrange("p (w h d) -> p w h d", w=2, d=D)).then_inc(v_ready, 1)
                exponentials(2)
                exponentials(3)
                if exists(a + 1):
                    turned(a + 1, (ai + 1) % TILES)

            def high_weights(e, n):
                w, h = (x[:, e].rearrange("p a c -> p (a c)") if n == "w3" else x[:, e, :] for x in (W[n], W[n + "h"]))
                act.mul(h, w, W_UP[n])
                act.mul(w, w, W_UP[n]).then_inc(w_high, 1)

            turned(0, 0)
            for t in (-3, -2, -1):
                step(t, t % TILES)
            act.wait_ge(loaded["w"][0], loaded["w"][1])
            with act.Fori(0, BATCH - 1) as b:
                for i in range(TILES):
                    step(b * TILES + i, i, (b, ("w1", "w2", "w3")[i]) if i < 3 else ())
            for i in range(TILES):
                step(NT - TILES + i, i, (BATCH - 1, ("w1", "w2", "w3")[i]) if i < 3 else ())

        @block.vector
        def _(dve):
            def chained(ins, value):
                ins.then_inc(dve_step, 1)
                dve.wait_ge(dve_step, value)

            def stats(t0, end):
                for t in range(t0, end):
                    dve.bn_stats(st[:, t, :], X[:, t, :]).then_inc(stats_ready, 1)
                dve.wait_ge(stats_ready, end)

            dve.memset(qs[:], 0.0).then_inc(start, 1)
            dve.memset(ks[:], 0.0).then_inc(start, 1)
            dve.wait_ge(x_first, 16)
            stats(0, PART)
            dve.memset(pad[:], 0.0)
            moments(dve, chained, st, mv, rstd, tmp, 0, PART, 0)

            def norm(n):
                dve.wait_ge(xT_up, n)
                dve.tensor_scalar(xn[:], X[:, n, :], mv[:, n, 0:1], rstd[:, n, :], ALU.subtract, ALU.mult).then_inc(xn_ready, 1)

            def rotate(a, ai):
                qk = psA[:, 0:256].rearrange("p (h a d) -> p h a d", a=2, d=4)
                crossed = rot_sin[:].rearrange("p (h a d) -> p h a d", a=2, d=4)
                cos = K["cos"][:, ai, :].unsqueeze(1).broadcast_to([P, 4 * H, 4])
                sin = K["sin"][:, ai, :].unsqueeze(1).broadcast_to([P, 2 * H, 4])
                nsin = K["nsin"][:, ai, :].unsqueeze(1).broadcast_to([P, 2 * H, 4])
                dve.wait_ge(qkv_up, a + 1)
                dve.wait_ge(hi_ready, a * 2)
                dve.tensor_tensor(rot_cos[:].rearrange("p (h d) -> p h d", d=4),
                                  psA[:, 0:256].rearrange("p (h d) -> p h d", d=4), cos, ALU.mult).then_inc(rope_ready, 1)
                dve.tensor_tensor(crossed[:, :, 0, :], qk[:, :, 1, :], sin, ALU.mult).then_inc(rope_ready, 1)
                dve.tensor_tensor(crossed[:, :, 1, :], qk[:, :, 0, :], nsin, ALU.mult).then_inc(rope_ready, 1)

            def step(t, i):
                c, n, ni, a = t + 1, t + 2, (i + 2) % TILES, t + 3
                ends, takes, scores = stages(t)
                if takes:
                    dve.wait_ge(q2_up, c + 1)
                    dve.tensor_copy(q2T[:], psQ).then_inc(q2_ready, 1)
                if ends:
                    y = psY[:].rearrange("p (r g d) -> p g r d", r=HG, d=ROWS)
                    dve.wait_ge(y_up, t + 1)
                    dve.reciprocal(rden[:].rearrange("p (g r) -> p g r", r=HG), y[:, :, :, D]).then_inc(rden_ready, 1)
                    dve.wait_ge(rden_ready, t + 1)
                    dve.tensor_tensor(yn[:].rearrange("p (g r d) -> p g r d", r=HG, d=D), y[:, :, :, 0:D],
                                      rden[:].rearrange("p (g r) -> p g r", r=HG).unsqueeze(3)
                                      .broadcast_to([P, HG, HG, D]), ALU.mult).then_inc(yn_ready, 1)
                if exists(a):
                    rotate(a, (i + 3) % TILES)
                if exists(a + 1):
                    norm(a + 1)
                if ends:
                    dve.wait_ge(out_up, t + 1)
                    dve.tensor_tensor(X[:, t, :], X[:, t, :], psT[:, 0:C], ALU.add).then_inc(x_done, 1)
                if ends:
                    dve.wait_ge(x_done, t + 1)
                    dve.bn_stats(st_out[:, t, :], X[:, t, :])
                if scores:
                    for r in range(HG):
                        dve.wait_ge(s1_up, n * HG + (r + 1))
                        dve.tensor_reduce(mx[:].rearrange("p (g r) -> p g r", r=HG)[:, :, r],
                                          psS[r][:].rearrange("p (g k) -> p g k", g=HG), AX_X, ALU.max).then_inc(s1_used, 1)
                    dve.wait_ge(s1_used, (n + 1) * HG)
                    dve.tensor_scalar(per_head(qs, ni)[:, :, HEADS], mx[:], -1.0, None, ALU.mult).then_inc(m_ready, 1)
                if takes:
                    dve.wait_ge(pv_up, c + 1)
                    dve.wait_ge(y_up, c)
                    dve.tensor_copy(yc[:], psY[:]).then_inc(yc_ready, 1)

            norm(0)
            dve.wait_ge(*loaded["a"])
            dve.tensor_copy(K["ident_bf"][:], K["ident"][:]).then_inc(made, 1)
            dve.tensor_copy(K["masks_bf"][:], K["masks"][:]).then_inc(made, 1)
            step(-3, 1)
            dve.wait_ge(x_rest, 16 * (NT // PART - 1))
            stats(PART, NT)
            dve.memset(pad[:], 0.0)
            step(-2, 2)
            moments(dve, chained, st, mv, rstd, tmp, PART, NT, MOMENT_LINKS)
            step(-1, 3)
            with dve.Fori(0, BATCH - 1) as b:
                for i in range(TILES):
                    step(b * TILES + i, i)
            for i in range(TILES):
                step(NT - TILES + i, i)

        @block.tensor
        def _(pe):
            pe.wait_ge(start, 7)
            pe.wait_ge(*loaded["a"])

            def masked(bank, mask):
                pe.matmul(bank[:], K["ident_bf"][:], mask.unsqueeze(1).broadcast_to([P, HG, P]), start=True, stop=True)

            def turn(n, t=None, c=None):
                pe.wait_ge(xn_ready, n + 1)
                if t is not None:
                    pe.wait_ge(x_done, t + 1)
                elif c is not None:
                    pe.wait_ge(q2_ready, c + 1)
                else:
                    pe.wait_ge(xT_ready, n)
                pe.transpose(psT[:, 0:P], xn[:], K["ident"][:]).then_inc(xT_up, 1)

            def step(t, i):
                ends, takes, scores = stages(t)
                c, ci, n, ni, a, ai = t + 1, (i + 1) % TILES, t + 2, (i + 2) % TILES, t + 3, (i + 3) % TILES
                if scores:
                    pe.wait_ge(lo_ready, (n + 1) * 2)
                    pe.wait_ge(qkT_ready, n)
                    for g in range(HG):
                        pe.transpose(psD[:, g, :], qs[:, ni, g * P:(g + 1) * P], K["ident16"][:])
                        last = pe.transpose(psD[:, HG + g, :], ks[:, ni, g * P:(g + 1) * P], K["ident16"][:])
                    last.then_inc(st_up, 1)
                own = xnT[:, PAD + ai * P:PAD + (ai + 1) * P]
                if exists(a):
                    pe.wait_ge(xT_ready, a + 1)
                    pe.wait_ge(rope_ready, a * 3)
                    pe.wait_ge(v_ready, a)
                    pe.matmul(psA[:, 0:256], own, W["qkvT"][:, 0:256], start=True, stop=True)
                elif ends:
                    pe.wait_ge(x_done, t)
                if takes:
                    pe.wait_ge(m_ready, c + 1)
                    for g in range(HG):
                        last = pe.transpose(psQ[:, g, :], qs[:, ci, g * P:(g + 1) * P], K["ident16"][:])
                    last.then_inc(q2_up, 1)
                if exists(a):
                    pe.matmul(psA[:, 256:384], xnT[:, ai * P:(ai + 1) * P], W["qkvT"][:, 256:384], start=True, stop=True)
                    pe.matmul(psA[:, 384:512], own, W["qkvT"][:, 256:384], start=True, stop=True).then_inc(qkv_up, 1)
                if ends:
                    pe.wait_ge(yc_ready, t + 1)
                    for r in range(HG):
                        last = pe.transpose(psY[:, r * P:(r + 1) * P], yc[:, r * P:(r + 1) * P], K["ident"][:])
                    last.then_inc(y_up, 1)

                def probabilities(r):
                    pe.wait_ge(q2_ready, c + 1)
                    pe.wait_ge(s1_used, c * HG + (r + 1))
                    masked(psS[r], K["mask_k"][:, 0 if ci == 0 else 1, :])
                    for g in range(HG):
                        for j in range(2):
                            w = 2 * ci + j
                            last = pe.matmul(psS[r][:, g * P + QB * j:g * P + QB * (j + 1)],
                                             qkT[ROWS * r:ROWS * r + HEADS + 1, HG + g, QB * w:QB * w + P],
                                             q2T[ROWS * r:ROWS * r + HEADS + 1, g, QB * j:QB * (j + 1)],
                                             start=False, stop=True, skip_group_check=True)
                    last.then_inc(s2_up, 1)

                def values(r):
                    pe.wait_ge(v_ready, c + 1)
                    pe.wait_ge(yn_ready, c)
                    pe.wait_ge(p_ready, c * HG + (r + 1))
                    for j in range(2):
                        for g in range(HG):
                            last = pe.matmul(psY[ROWS * g:ROWS * (g + 1), r * P + QB * j:r * P + QB * (j + 1)],
                                             v_sb[:, 2 * ci + j, HG * g + r, :],
                                             prob[:, r, g * P + QB * j:g * P + QB * (j + 1)], start=True, stop=True)
                    if r == HG - 1:
                        last.then_inc(pv_up, 1)

                def maxima(r):
                    pe.wait_ge(qkT_ready, n + 1)
                    if takes:
                        pe.wait_ge(p_ready, c * HG + (r + 1))
                    masked(psS[r], K["mask_q"][:, 0 if ni == 0 else 1, :])
                    for g in range(HG):
                        for j in range(2):
                            w = 2 * ni + j
                            last = pe.matmul(psS[r][QB * j:QB * (j + 1), g * P:(g + 1) * P],
                                             qkT[ROWS * r:ROWS * r + HEADS, g, PAD + QB * w:PAD + QB * (w + 1)],
                                             qkT[ROWS * r:ROWS * r + HEADS, HG + g, QB * w:QB * w + P],
                                             start=False, stop=True, skip_group_check=True)
                    last.then_inc(s1_up, 1)

                if takes:
                    probabilities(0)
                    probabilities(1)
                if ends:
                    pe.wait_ge(yn_ready, t + 1)
                    if takes:
                        pe.wait_ge(q2_ready, c + 1)
                    pe.transpose(psT[:, 0:P], yn[:], K["ident"][:]).then_inc(yT_up, 1)
                for r in range(HG):
                    if takes and r < HG - 1:
                        values(r)
                    if scores:
                        maxima(r)
                    if r == 0 and ends:
                        pe.wait_ge(yT_ready, t + 1)
                        pe.matmul(psT[:, 0:C], yT[:], W["projT"][:], start=True, stop=True).then_inc(out_up, 1)
                    if takes and r < HG - 2:
                        probabilities(r + 2)
                if exists(a + 1):
                    turn(a + 1, t if ends else None, c if takes else None)
                if takes:
                    values(HG - 1)

            turn(0)
            step(-3, 1)
            pe.wait_ge(made, 2)
            step(-2, 2)
            step(-1, 3)
            with pe.Fori(0, BATCH - 1) as b:
                for i in range(TILES):
                    step(b * TILES + i, i)
            for i in range(TILES):
                step(NT - TILES + i, i)


def mixture(nc, sb, psum, sem, X, K, W, tag, st, st_out=None, x_out=None):
    pad = sb(tag + "pad", [P, 1], F32)
    mv = sb(tag + "mv", [P, NT, 2], F32)
    rstd = sb(tag + "rstd", [P, NT, 1], F32)
    tmp = sb(tag + "tmp", [P, NT], F32)
    xn = sb(tag + "xn", [P, TILES, C], F32)
    xnT = sb(tag + "xnT", [P, T], F32)
    xh = sb(tag + "xh", [P, 2, T], F16)
    xl = sb(tag + "xl", [P, 2, T], F16)
    lg = sb(tag + "lg", [P, TILES, E], F32)
    top = sb(tag + "top", [P, TILES, 8], F32)
    idx = sb(tag + "idx", [P, TILES, 8], U32)
    idf = sb(tag + "idf", [P, TILES, 2], F32)
    gap = sb(tag + "gap", [P, TILES], F32)
    th = sb(tag + "th", [P, TILES], F32)
    w12 = sb(tag + "w12", [P, TILES, 2], F32)
    pick = sb(tag + "pick", [P, TILES, 2, E], F32)
    gate = sb(tag + "gate", [P, 2, TILES, E], F32)
    su = sb(tag + "su", [P, 2, T], F32)
    hf = sb(tag + "hf", [P, 2, T], F32)
    hh = sb(tag + "hh", [P, 4, T], F16)
    hl = sb(tag + "hl", [P, 4, T], F16)

    psU = [psum(f"{tag}psU{i}", [P, 512], F32) for i in range(2)]
    psV = [psum(f"{tag}psV{i}", [P, 512], F32) for i in range(2)]
    psY = [psum(f"{tag}psY{i}", [P, 512], F32) for i in range(2)]
    psT = psum(tag + "psT", [P, 512], F32)
    psL = psum(tag + "psL", [P, 512], F32)

    xn_ready = sem(tag + "xn_ready")
    xT_up = sem(tag + "xT_up")
    xT_ready = sem(tag + "xT_ready")
    xl_ready = sem(tag + "xl_ready")
    lg_up = sem(tag + "lg_up")
    gap_ready = sem(tag + "gap_ready")
    th_ready = sem(tag + "th_ready")
    u_up = sem(tag + "u_up")
    v_up = sem(tag + "v_up")
    su_ready = sem(tag + "su_ready")
    h_ready = sem(tag + "h_ready")
    hh_ready = sem(tag + "hh_ready")
    hl_ready = sem(tag + "hl_ready")
    y_up = sem(tag + "y_up")
    y_used = sem(tag + "y_used")
    dve_step = sem(tag + "dve_step")
    stored = sem(tag + "stored")
    FRONT = 9
    UNITS = E * HC
    NORM, TURN, LOGITS, GATES = 1, 2, 3, 6

    def rows(eng, row):
        with eng.Fori(0, BATCH // 2 - 1) as b2:
            for half in range(2):
                row(b2 * 2 + half, half)
        for b in range(BATCH - 2, BATCH):
            row(b, b % 2)

    def follows(b):
        return not isinstance(b, int) or b < BATCH - 1

    with nc.Block() as block:

        @block.vector
        def _(dve):
            dve.sem_inc(y_used, 2)

            def chained(ins, value):
                ins.then_inc(dve_step, 1)
                dve.wait_ge(dve_step, value)

            def norms(b):
                dve.wait_ge(xT_up, b)
                for i in range(TILES):
                    t = b * TILES + i
                    ins = dve.tensor_scalar(xn[:, i, :], X[:, t, :], mv[:, t, 0:1], rstd[:, t, :],
                                            ALU.subtract, ALU.mult)
                ins.then_inc(xn_ready, 1)

            def choose(b):
                s0 = b * FRONT + STAT_LINKS
                dve.wait_ge(lg_up, b + 1)
                chained(dve.tensor_copy(lg[:], psL[:, 0:TILES * E].rearrange("p (i e) -> p i e", e=E)), s0 + 1)
                dve.memset(pad[:], 0.0)
                for i in range(TILES):
                    ins = dve.max(top[:, i, :], lg[:, i, :])
                chained(ins, s0 + 2)
                dve.tensor_tensor(gap[:], top[:, :, 0], top[:, :, 1], ALU.subtract).then_inc(gap_ready, 1)
                for i in range(TILES):
                    ins = dve.max_index(idx[:, i, :], top[:, i, :], lg[:, i, :])
                chained(ins, s0 + 3)
                chained(dve.tensor_copy(idf[:], idx[:, :, 0:2]), s0 + 4)

            def gates(b, slot):
                s0 = b * FRONT + STAT_LINKS
                dve.wait_ge(th_ready, b + 1)
                half = 0.5 / Y_UP
                chained(dve.tensor_scalar(w12[:, :, 0], th[:], half, half, ALU.mult, ALU.add), s0 + 5)
                chained(dve.tensor_scalar(w12[:, :, 1], th[:], -half, half, ALU.mult, ALU.add), s0 + 6)
                every = [P, TILES, 2, E]
                chained(dve.tensor_tensor(pick[:], K["iota"][:].unsqueeze(1).unsqueeze(1).broadcast_to(every),
                                          idf[:].unsqueeze(3).broadcast_to(every), ALU.is_equal), s0 + 7)
                chained(dve.tensor_tensor(pick[:], pick[:], w12[:].unsqueeze(3).broadcast_to(every), ALU.mult), s0 + 8)
                chained(dve.tensor_tensor(gate[:, slot, :, :], pick[:, :, 0, :], pick[:, :, 1, :], ALU.add), s0 + 9)

            def hidden(b, n):
                dve.wait_ge(su_ready, b * UNITS + (n + 1))
                dve.wait_ge(v_up, b * UNITS + (n + 1))
                if n >= 2:
                    dve.wait_ge(hl_ready, b * UNITS + (n - 1))
                dve.tensor_tensor(hf[:, n % 2, :], su[:, n % 2, :], psV[n % 2][:], ALU.mult).then_inc(h_ready, 1)

            def collect(b, e, slot):
                dve.wait_ge(y_up, b * E + (e + 1))
                dve.wait_ge(y_used, b * E + (e + 2))
                for i in range(TILES):
                    ins = dve.scalar_tensor_tensor(X[:, b * TILES + i, :], psY[e % 2][:, i * P:(i + 1) * P],
                                                   gate[:, slot, i, e:e + 1], X[:, b * TILES + i, :],
                                                   ALU.mult, ALU.add)
                ins.then_inc(y_used, 1)

            moments(dve, chained, st, mv, rstd, tmp, 0, TILES, 0)
            norms(0)
            moments(dve, chained, st, mv, rstd, tmp, TILES, NT, MOMENT_LINKS)
            choose(0)
            gates(0, 0)
            for n in range(HC):
                hidden(0, n)

            def row(b, half):
                for e in range(E):
                    if follows(b) or e < E - 1:
                        for c in range(HC):
                            hidden(b, (e + 1) * HC + c)
                    collect(b, e, half)
                    if follows(b):
                        if e == NORM - 1:
                            norms(b + 1)
                        if e == LOGITS + 1:
                            choose(b + 1)
                        if e == GATES:
                            gates(b + 1, (half + 1) % 2)
                if st_out is not None:
                    dve.wait_ge(y_used, b * E + (E + 2))
                    for i in range(TILES):
                        dve.bn_stats(st_out[:, b * TILES + i, :], X[:, b * TILES + i, :])

            rows(dve, row)

        @block.gpsimd
        def _(pool):
            def low_x(b, slot):
                pool.wait_ge(xT_ready, b * 2 + 2)
                pool.tensor_tensor(xl[:, slot, :], xnT[:], xh[:, slot, :], ALU.subtract).then_inc(xl_ready, 1)

            def low(b, n):
                pool.wait_ge(hh_ready, b * UNITS + (n + 1))
                pool.tensor_tensor(hl[:, n % 4, :], hf[:, n % 2, :], hh[:, n % 4, :], ALU.subtract).then_inc(hl_ready, 1)

            low_x(0, 0)
            for n in range(HC):
                low(0, n)

            def row(b, half):
                for e in range(E):
                    if follows(b) or e < E - 1:
                        for c in range(HC):
                            low(b, (e + 1) * HC + c)
                    if follows(b) and e == TURN:
                        low_x(b + 1, (half + 1) % 2)

            rows(pool, row)

        @block.scalar
        def _(act):
            def turned(b, slot):
                act.wait_ge(xT_up, b + 1)
                act.wait_ge(xl_ready, b)
                act.copy(xnT[:], psT[:]).then_inc(xT_ready, 1)
                act.copy(xh[:, slot, :], psT[:]).then_inc(xT_ready, 1)

            def gap_tanh(b):
                act.wait_ge(gap_ready, b + 1)
                act.activation(th[:], gap[:], ACT.Tanh, scale=0.5).then_inc(th_ready, 1)

            def silu(b, n):
                act.wait_ge(u_up, b * UNITS + (n + 1))
                if n >= 2:
                    act.wait_ge(h_ready, b * UNITS + (n - 1))
                act.activation(su[:, n % 2, :], psU[n % 2][:], ACT.Silu, scale=1.0 / W_UP["w1"]).then_inc(su_ready, 1)

            def high(b, n):
                act.wait_ge(h_ready, b * UNITS + (n + 1))
                if n >= 4:
                    act.wait_ge(y_up, b * E + (n // HC - 1))
                act.copy(hh[:, n % 4, :], hf[:, n % 2, :]).then_inc(hh_ready, 1)

            turned(0, 0)
            gap_tanh(0)
            for n in range(HC):
                silu(0, n)
                high(0, n)

            def row(b, half):
                for e in range(E):
                    if follows(b) or e < E - 1:
                        for c in range(HC):
                            silu(b, (e + 1) * HC + c)
                        for c in range(HC):
                            high(b, (e + 1) * HC + c)
                    if follows(b):
                        if e == TURN:
                            turned(b + 1, (half + 1) % 2)
                        if e == LOGITS + 2:
                            gap_tanh(b + 1)

            rows(act, row)

        @block.tensor
        def _(pe):
            def turn(b):
                pe.wait_ge(xn_ready, b + 1)
                for i in range(TILES):
                    ins = pe.transpose(psT[:, i * P:(i + 1) * P], xn[:, i, :], K["ident"][:])
                ins.then_inc(xT_up, 1)

            def logits(b):
                pe.wait_ge(xT_ready, b * 2 + 1)
                for i in range(TILES):
                    ins = pe.matmul(psL[:, i * E:(i + 1) * E], xnT[:, i * P:(i + 1) * P], W["g"][:], start=True, stop=True)
                ins.then_inc(lg_up, 1)

            def thrice(out, wh, wl, slot):
                pe.matmul(out, wh, xh[:, slot, :], start=True, stop=False)
                pe.matmul(out, wh, xl[:, slot, :], start=False, stop=False)
                return pe.matmul(out, wl, xh[:, slot, :], start=False, stop=True)

            def up(b, e, slot):
                for c in range(HC):
                    n, ee, cols = e * HC + c, e % E, slice(c * P, (c + 1) * P)
                    if n >= 2:
                        pe.wait_ge(su_ready, b * UNITS + (n - 1))
                    thrice(psU[n % 2][:], W["w1h"][:, ee, cols], W["w1l"][:, ee, cols], slot).then_inc(u_up, 1)
                    if n >= 2:
                        pe.wait_ge(h_ready, b * UNITS + (n - 1))
                    thrice(psV[n % 2][:], W["w2h"][:, ee, cols], W["w2l"][:, ee, cols], slot).then_inc(v_up, 1)

            def down(b, e):
                pe.wait_ge(hl_ready, b * UNITS + (e + 1) * HC)
                pe.wait_ge(y_used, b * E + (e + 1))
                for i in range(TILES):
                    out = psY[e % 2][:, i * P:(i + 1) * P]
                    for c in range(HC):
                        s, tok = (e * HC + c) % 4, slice(i * P, (i + 1) * P)
                        pe.matmul(out, hh[:, s, tok], W["w3h"][:, e, c, :], start=(c == 0), stop=False)
                        pe.matmul(out, hh[:, s, tok], W["w3l"][:, e, c, :], start=False, stop=False)
                        ins = pe.matmul(out, hl[:, s, tok], W["w3h"][:, e, c, :], start=False, stop=(c == HC - 1))
                ins.then_inc(y_up, 1)

            turn(0)
            logits(0)
            pe.wait_ge(xl_ready, 1)
            up(0, 0, 0)

            def row(b, half):
                for e in range(E):
                    if e < E - 1:
                        up(b, e + 1, half)
                    elif follows(b):
                        pe.wait_ge(xl_ready, b + 2)
                        up(b, E, (half + 1) % 2)
                    down(b, e)
                    if follows(b):
                        if e == TURN - 1:
                            turn(b + 1)
                        if e == LOGITS:
                            logits(b + 1)

            rows(pe, row)

        if x_out is not None:
            @block.sync
            def _(sp):
                with sp.Fori(0, BATCH) as b:
                    sp.wait_ge(y_used, b * E + (E + 2))
                    sp.dma_start(x_out[:, bass.ds(b * TILES, TILES), :], X[:, bass.ds(b * TILES, TILES), :]).then_inc(stored, 16)
                sp.wait_ge(stored, 16 * BATCH)


def log_factors():
    roots = np.roots(LOG_POLY[::-1])
    real = [r.real for r in roots if abs(r.imag) < 1e-9]
    pairs = [(r.real, r.imag ** 2) for r in roots if r.imag > 1e-9]
    assert len(real) == 1 and len(pairs) == 2
    return float(LOG_POLY[-1]), float(real[0]), [(float(a), float(b)) for a, b in pairs]


def scan(nc, sb, psum, sem, X, K, W, loaded, st, st_out):
    mv = sb("s_mv", [P, NT, 2], F32)
    rstd = sb("s_rstd", [P, NT, 1], F32)
    tmp = sb("s_tmp", [P, NT], F32)
    xn = sb("s_xn", [P, TILES, C], F32)
    xnT = sb("s_xnT", [P, 2, T], F32)
    rT = sb("s_rT", [RANK, T], F32)
    ez = sb("s_ez", [P, T], F32)
    sq = sb("s_sq", [P, 2, T], F32)
    lp = sb("s_lp", [P, T], F32)
    dlt = sb("s_dlt", [P, T], F32)
    dx = sb("s_dx", [P, T], F32)
    halves = sb("s_halves", [P, 4, T], F16)
    spreads = sb("s_spreads", [P, 2, QUARTERS, T], F16)
    Brep = sb("s_Brep", [P, 2, T], F32)
    Crep = sb("s_Crep", [P, 2, T], F32)
    abar = sb("s_abar", [P, 4, T], F32)
    dbx = sb("s_dbx", [P, 4, T], F32)
    hst = sb("s_hst", [P, 8, T], F32)
    hc = sb("s_hc", [P, 8, T], F32)
    yT = sb("s_yT", [P, T], F32)
    lead, root, pairs = log_factors()
    D_diag = sb("s_D_diag", [P, P], F32)
    shift = sb("s_shift", [P, 3], F32)

    psE = [psum(f"s_psE{i}", [P, 512], F32) for i in range(2)]
    psX = [psum(f"s_psX{i}", [P, 512], F32) for i in range(4)]
    psY = psum("s_psY", [P, 512], F32)
    psT = psum("s_psT", [P, 512], F32)

    A_ready = sem("s_A_ready")
    made = sem("s_made")
    centred = sem("s_centred")
    xn_ready = sem("s_xn_ready")
    xT_up = sem("s_xT_up")
    xT_ready = sem("s_xT_ready")
    proj_up = sem("s_proj_up")
    proj_used = sem("s_proj_used")
    sq_ready = sem("s_sq_ready")
    hi_ready = sem("s_hi_ready")
    lo_ready = sem("s_lo_ready")
    spreads_ready = sem("s_spreads_ready")
    e_up = sem("s_e_up")
    x_up = sem("s_x_up")
    a_ready = sem("s_a_ready")
    dbx_ready = sem("s_dbx_ready")
    h_ready = sem("s_h_ready")
    hc_ready = sem("s_hc_ready")
    gathered = sem("s_gathered")
    y_ready = sem("s_y_ready")
    o_up = sem("s_o_up")
    x_done = sem("s_x_done")
    dve_step = sem("s_dve_step")
    LINKS = 6
    MOVES = 16 * 4 * QUARTERS
    LAG = 6
    Y, OUT, ADD = G + LAG, G + LAG + 1, G + LAG + 1
    BODY = {"norm": 8, "turn": 13, "r": 14, "z": 15, "squares": 17, "deltas": (14, 17, 18, 19), "high": (20, 21), "low": 20, "B": 18, "C": 19}
    HEAD = {"norm": 0, "turn": 1, "r": 2, "z": 3, "squares": 3, "deltas": (3, 4, 5, 6), "high": (6, 7), "low": 7, "B": 4, "C": 5}
    FIRST = ADD + 1 - G
    assert FIRST == BODY["norm"] and FIRST > HEAD["low"]

    def turns(eng, steps):
        steps(0, 0, 0, FIRST, 1, HEAD)
        with eng.Fori(0, BATCH // 2 - 1) as b2:
            for half in range(2):
                steps(b2 * 2 + half, half, FIRST, G + FIRST, b2 * 2 + (half + 2), BODY)
        steps(BATCH - 2, 0, FIRST, G + FIRST, None, {})
        steps(BATCH - 1, 1, FIRST, G + FIRST, None, {})

    def has(b, g):
        return not isinstance(b, int) or b * G + g < BATCH * G

    with nc.Block() as block:

        @block.vector
        def _(dve):
            dve.memset(shift[:, 0:1], -pairs[0][0])
            dve.memset(shift[:, 1:2], -pairs[1][0])
            dve.memset(shift[:, 2:3], pairs[1][1])
            dve.wait_ge(*loaded["s"])
            dve.tensor_scalar(D_diag[:], K["ident"][:], W["D"][:], None, ALU.mult).then_inc(made, 1)

            def chained(ins, value):
                ins.then_inc(dve_step, 1)
                dve.wait_ge(dve_step, value)

            def deltas(b, slot, k):
                at = STAT_LINKS + b * LINKS
                if k == 0:
                    dve.wait_ge(proj_used, b * 4 + 2)
                    chained(dve.tensor_scalar(ez[:], ez[:], E_MAX, None, ALU.min), at + 1)
                elif k == 1:
                    dve.wait_ge(sq_ready, b * 2 + 2)
                    chained(dve.scalar_tensor_tensor(lp[:], sq[:, 0, :], pairs[0][1], sq[:, 1, :], ALU.add, ALU.mult), at + 2)
                    chained(dve.scalar_tensor_tensor(lp[:], ez[:], -root, lp[:], ALU.add, ALU.mult), at + 3)
                elif k == 2:
                    dve.wait_ge(lo_ready, b * 2)
                    chained(dve.scalar_tensor_tensor(lp[:], lp[:], UP * lead, ez[:], ALU.mult, ALU.mult), at + 4)
                    chained(dve.tensor_scalar(dlt[:], lp[:], UP * DT_MIN, UP * DT_MAX, ALU.max, ALU.min), at + 5)
                else:
                    dve.wait_ge(xT_ready, b + 1)
                    chained(dve.tensor_tensor(dx[:], dlt[:], xnT[:, slot, :], ALU.mult), at + 6)

            def drive(b, g, slot):
                dve.wait_ge(x_up, b * G + (g + 1))
                if g % G == 0:
                    dve.wait_ge(proj_used, b * 4 + (g // G * 4 + 3))
                if g >= 4:
                    dve.wait_ge(h_ready, b * G + (g - 3))
                dve.tensor_tensor(dbx[:, g % 4, :], psX[g % 4][:], Brep[:, slot, :], ALU.mult).then_inc(dbx_ready, 1)

            def states(b, g):
                dve.wait_ge(a_ready, b * G + (g + 1))
                dve.wait_ge(dbx_ready, b * G + (g + 1))
                if g >= 8:
                    dve.wait_ge(hc_ready, b * G + (g - 7))
                dve.tensor_tensor_scan(hst[:, g % 8, :], abar[:, g % 4, :], dbx[:, g % 4, :], 0.0,
                                       ALU.mult, ALU.add).then_inc(h_ready, 1)

            def steps(b, half, first, end, n, at):
                for g in range(first, end):
                    if has(b, g):
                        drive(b, g, (half + g // G) % 2)
                    if g >= 1 and has(b, g - 1):
                        states(b, g - 1)
                    if g in at.get("deltas", ()):
                        deltas(n, (half if first else 1), at["deltas"].index(g))
                    if g == ADD:
                        dve.wait_ge(o_up, b + 1)
                        rows = X[:, bass.ds(b * TILES, TILES), :]
                        dve.tensor_tensor(rows, rows, psT[:].rearrange("p (i c) -> p i c", c=C), ALU.add).then_inc(x_done, 1)
                        dve.wait_ge(x_done, b + 2)
                        for i in range(TILES):
                            dve.bn_stats(st_out[:, b * TILES + i, :], X[:, b * TILES + i, :])

            moments(dve, chained, st, mv, rstd, tmp, 0, TILES, 0)
            for i in range(TILES):
                ins = dve.tensor_scalar(xn[:, i, :], X[:, i, :], mv[:, i, 0:1], rstd[:, i, :], ALU.subtract, ALU.mult)
            ins.then_inc(xn_ready, 1)
            dve.sem_inc(x_done, 1)
            dve.wait_ge(A_ready, 1)
            dve.tensor_scalar(W["A"][:], W["A"][:], -1.0 / UP, None, ALU.mult).then_inc(A_ready, 1)
            moments(dve, chained, st, mv, rstd, tmp, TILES, NT, MOMENT_LINKS)
            for k in range(4):
                deltas(0, 0, k)
            dve.wait_ge(hi_ready, 2)
            for n, whole in enumerate((dlt, dx)):
                dve.tensor_tensor(halves[:, 2 * n + 1, :], whole[:], halves[:, 2 * n, :], ALU.subtract).then_inc(lo_ready, 1)
            turns(dve, steps)

        @block.gpsimd
        def _(pool):
            def norms(b):
                rows, every = bass.ds(b * TILES, TILES), [P, TILES, C]
                pool.wait_ge(xT_up, b)
                pool.tensor_tensor(xn[:], X[:, rows, :], mv[:, rows, 0:1].broadcast_to(every), ALU.subtract).then_inc(centred, 1)
                pool.wait_ge(centred, b)
                pool.tensor_tensor(xn[:], xn[:], rstd[:, rows, :].broadcast_to(every), ALU.mult).then_inc(xn_ready, 1)

            def low(b):
                pool.wait_ge(hi_ready, b * 2 + 2)
                pool.wait_ge(dve_step, STAT_LINKS + b * LINKS + 6)
                pool.wait_ge(spreads_ready, b * MOVES)
                for n, whole in enumerate((dlt, dx)):
                    pool.tensor_tensor(halves[:, 2 * n + 1, :], whole[:], halves[:, 2 * n, :], ALU.subtract).then_inc(lo_ready, 1)

            def steps(b, half, first, end, n, at):
                for g in range(first, end):
                    if g == at.get("norm"):
                        norms(n)
                    if g == at.get("low"):
                        low(n)
                    if not has(b, g):
                        continue
                    pool.wait_ge(h_ready, b * G + (g + 1))
                    if g % G == 0:
                        pool.wait_ge(proj_used, b * 4 + (g // G * 4 + 4))
                    if g >= 8:
                        pool.wait_ge(gathered, b * SUBS + (g // QUARTERS - 1))
                    pool.tensor_tensor(hc[:, g % 8, :], hst[:, g % 8, :], Crep[:, (half + g // G) % 2, :],
                                       ALU.mult).then_inc(hc_ready, 1)

            pool.wait_ge(dve_step, STAT_LINKS)
            turns(pool, steps)

        @block.sync
        def _(sp):
            def move(b, slot):
                for n, ready, count in ((0, hi_ready, 1), (2, hi_ready, 2), (1, lo_ready, 1), (3, lo_ready, 2)):
                    sp.wait_ge(ready, b * 2 + count)
                    for q in range(QUARTERS):
                        sp.dma_start(spreads[QUARTER * n:QUARTER * (n + 1), slot, q, :],
                                     halves[QUARTER * q:QUARTER * (q + 1), n, :]).then_inc(spreads_ready, 16)

            move(0, 0)
            with sp.Fori(0, BATCH // 2 - 1) as b2:
                for half in range(2):
                    move(b2 * 2 + (half + 1), (half + 1) % 2)
            move(BATCH - 1, 1)
            sp.wait_ge(spreads_ready, BATCH * MOVES)

        @block.scalar
        def _(act):
            act.wait_ge(*loaded["s"])
            act.activation(W["A"][:], W["A"][:], ACT.Exp).then_inc(A_ready, 1)
            act.sem_inc(y_ready, 1)

            def turned(b, slot):
                act.wait_ge(xT_up, b + 1)
                act.copy(xnT[:, slot, :], psT[:]).then_inc(xT_ready, 1)

            def projected(b, slot, k):
                act.wait_ge(proj_up, b * 4 + (k + 1))
                if k == 0:
                    ins = act.copy(rT[:], psT[0:RANK, :])
                elif k == 1:
                    act.wait_ge(lo_ready, b * 2)
                    ins = act.activation(ez[:], psT[:], ACT.Exp, bias=W["dtb"][:])
                elif k == 2:
                    ins = act.mul(Brep[:, slot, :], psT[:], 1.0 / UP)
                else:
                    ins = act.copy(Crep[:, slot, :], psT[:])
                ins.then_inc(proj_used, 1)

            def squares(b):
                act.wait_ge(dve_step, STAT_LINKS + b * LINKS + 1)
                act.wait_ge(made, 1)
                act.activation(sq[:, 0, :], ez[:], ACT.Square, bias=shift[:, 0:1])
                act.activation(sq[:, 1, :], ez[:], ACT.Square, bias=shift[:, 1:2]).then_inc(sq_ready, 1)
                act.wait_ge(sq_ready, b * 2 + 1)
                act.activation(sq[:, 1, :], sq[:, 1, :], ACT.Identity, bias=shift[:, 2:3]).then_inc(sq_ready, 1)

            def high(b, n):
                act.wait_ge(dve_step, STAT_LINKS + b * LINKS + 5 + n)
                act.wait_ge(spreads_ready, b * MOVES)
                act.copy(halves[:, 2 * n, :], (dlt, dx)[n][:]).then_inc(hi_ready, 1)

            def steps(b, half, first, end, n, at):
                slot = (half if first else 1)
                for g in range(first, end):
                    if has(b, g):
                        act.wait_ge(e_up, b * G + (g + 1))
                        if g >= 4:
                            act.wait_ge(h_ready, b * G + (g - 3))
                        act.activation(abar[:, g % 4, :], psE[g % 2][:], ACT.Exp, scale=W["A"][:, g % G:g % G + 1]).then_inc(a_ready, 1)
                    if g == at.get("turn"):
                        if first:
                            act.wait_ge(gathered, b * SUBS + 1)
                        turned(n, slot)
                    for k, part in enumerate(("r", "z", "B", "C")):
                        if g == at.get(part):
                            if first and part == "C":
                                act.wait_ge(hc_ready, b * G + G)
                            projected(n, slot, k)
                    if g == at.get("squares"):
                        squares(n)
                    if g in at.get("high", ()):
                        high(n, at["high"].index(g))
                    if g == Y:
                        act.wait_ge(gathered, b * SUBS + SUBS)
                        act.copy(yT[:], psY[:]).then_inc(y_ready, 1)

            turned(0, 0)
            projected(0, 0, 0)
            projected(0, 0, 1)
            squares(0)
            projected(0, 0, 2)
            high(0, 0)
            high(0, 1)
            projected(0, 0, 3)
            act.wait_ge(A_ready, 2)
            turns(act, steps)

        @block.tensor
        def _(pe):
            pe.wait_ge(*loaded["s"])
            pe.wait_ge(made, 1)

            def turn(b, o=None):
                pe.wait_ge(xn_ready, b + 1)
                if o is not None:
                    pe.wait_ge(x_done, o + 1)
                else:
                    pe.wait_ge(proj_used, b * 4)
                for i in range(TILES):
                    ins = pe.transpose(psT[:, i * P:(i + 1) * P], xn[:, i, :], K["ident"][:])
                ins.then_inc(xT_up, 1)

            def project(b, slot, k):
                if k == 0:
                    pe.wait_ge(xT_ready, b + 1)
                pe.wait_ge(proj_used, b * 4 + k)
                if k == 0:
                    ins = pe.matmul(psT[0:RANK, :], W["xpT"][:], xnT[:, slot, :], start=True, stop=True)
                elif k == 1:
                    ins = pe.matmul(psT[:], W["dtT"][:], rT[:], start=True, stop=True)
                else:
                    ins = pe.matmul(psT[:], W["BT" if k == 2 else "CT"][:], xnT[:, slot, :], start=True, stop=True)
                ins.then_inc(proj_up, 1)

            def spread(b, g, slot):
                q, sub = g % QUARTERS, g % G // QUARTERS
                if g % G == 0:
                    pe.wait_ge(spreads_ready, (b + (g // G + 1)) * MOVES)
                if g >= 2:
                    pe.wait_ge(a_ready, b * G + (g - 1))
                if g >= 4:
                    pe.wait_ge(dbx_ready, b * G + (g - 3))
                for rows, bank, up in ((slice(0, P // 2), psE[g % 2], e_up), (slice(P // 2, P), psX[g % 4], x_up)):
                    pe.matmul(bank[:], K["sel"][rows, sub * P:(sub + 1) * P], spreads[rows, slot, q, :],
                              start=True, stop=True).then_inc(up, 1)

            def gather(b, g, slot):
                pe.wait_ge(hc_ready, b * G + (g + QUARTERS))
                if g % G == 0:
                    pe.wait_ge(y_ready, b + (g // G + 1))
                    pe.matmul(psY[:], D_diag[:], xnT[:, slot, :], start=True, stop=True)
                for k in range(g, g + QUARTERS):
                    q, sub = k % QUARTERS, k % G // QUARTERS
                    ins = pe.matmul(psY[QUARTER * q:QUARTER * (q + 1), :], K["selT"][:, sub * QUARTER:(sub + 1) * QUARTER],
                                    hc[:, k % 8, :], start=False, stop=True, skip_group_check=True)
                ins.then_inc(gathered, 1)

            def steps(b, half, first, end, n, at):
                for g in range(first, end):
                    if has(b, g):
                        spread(b, g, (half + g // G) % 2)
                    k = g - LAG
                    if k >= 0 and k % QUARTERS == QUARTERS - 1 and has(b, k):
                        gather(b, k - (QUARTERS - 1), (half + k // G) % 2)
                    if g == at.get("turn"):
                        turn(n, b if first else None)
                    for k, part in enumerate(("r", "z", "B", "C")):
                        if g == at.get(part):
                            project(n, (half if first else 1), k)
                    if g == OUT:
                        pe.wait_ge(y_ready, b + 2)
                        if n is not None:
                            pe.wait_ge(proj_used, (b + 3) * 4)
                        for i in range(TILES):
                            ins = pe.transpose(psT[:, i * P:(i + 1) * P], yT[:, i * P:(i + 1) * P], K["ident"][:])
                        ins.then_inc(o_up, 1)

            turn(0)
            for k in range(4):
                project(0, 0, k)
            turns(pe, steps)


def build(nc, x_in, x_out, dram, phases=4):
    with ExitStack() as outer:
        def keep(name, shape, dt):
            return outer.enter_context(nc.sbuf_tensor(name, shape, dt))

        def sem(name):
            return outer.enter_context(nc.semaphore(name))

        X = keep("X", [P, NT, C], F32)
        K = {n: keep("k_" + n, list(s), dt) for n, s, dt in (
            ("ident", (P, P), F32), ("ident16", (P, P), F16), ("masks", (P, 2, 2, P), F32),
            ("cos", (P, TILES, 4), F32), ("sin", (P, TILES, 4), F32), ("nsin", (P, TILES, 4), F32),
            ("iota", (P, E), F32), ("sel", (P, SUBS * P), F16), ("selT", (P, SUBS * QUARTER), F32))}
        ident_bf = keep("ident_bf", [P, P], BF16)
        masks_bf = keep("masks_bf", [P, 2, 2, P], BF16)
        W = {n: keep("w_" + n, list(s), F32) for n, s in (
            ("qkvT", (P, 3 * C)), ("projT", (P, C)), ("g", (P, E)), ("w1", (P, E, HID)), ("w2", (P, E, HID)),
            ("w3", (P, E, HC, C)), ("A", (P, G)), ("D", (P, 1)), ("dtb", (P, 1)), ("xpT", (P, RANK)),
            ("dtT", (RANK, P)), ("BT", (P, P)), ("CT", (P, P)))}
        for n, s in (("w1", (P, E, HID)), ("w2", (P, E, HID)), ("w3", (P, E, HC, C))):
            for half in "hl":
                W[n + half] = keep("w_" + n + half, list(s), F16)

        groups = {
            "a": ("ident", "masks", "ident16", "qkvT", "cos", "sin", "nsin", "projT"),
            "w": ("w1", "w2", "w3", "g", "iota"),
            "s": ("A", "D", "dtb", "xpT", "dtT", "BT", "CT", "sel", "selT"),
        }
        loaded = {g: (sem("loaded_" + g), 16 * len(names)) for g, names in groups.items()}
        st = [keep(f"st{k}", [P, NT, 6], F32) for k in range(2)]
        K["ident_bf"] = ident_bf
        K["masks_bf"], K["mask_q"], K["mask_k"] = masks_bf, masks_bf[:, 0], masks_bf[:, 1]

        def stage(n, fn, *args):
            if phases < n:
                return
            with ExitStack() as ctx:
                def sb(name, shape, dt):
                    return ctx.enter_context(nc.sbuf_tensor(name, shape, dt))

                def psum(name, shape, dt):
                    return ctx.enter_context(nc.psum_tensor(name, shape, dt))
                fn(nc, sb, psum, sem, X, K, W, *args)

        xo = x_out.rearrange("(t p) c -> p t c", p=P)
        stage(1, attention, x_in, dram, groups, loaded, st[0])
        stage(2, mixture, "f_", st[0], st[1])
        stage(3, scan, loaded, st[1], st[0])
        stage(4, mixture, "g_", st[0], None, xo)
        if phases < 4:
            stored = sem("stored")
            with nc.Block() as block:
                @block.sync
                def _(sp):
                    sp.dma_start(xo, X[:, 0:NT, :]).then_inc(stored, 16)
                    sp.wait_ge(stored, 16)


def constants():
    f = np.float32
    inv = (1.0 / np.float32(10000.0) ** (np.arange(0, D, 2, dtype=f) / f(D))).astype(f)
    ang = np.outer(np.arange(T, dtype=f), inv).astype(f).reshape(TILES, P, 4).transpose(1, 0, 2)
    p = np.arange(P)[:, None]
    k = np.arange(P)[None, :]
    q = p % QB
    ok = (k >= q) & (k <= q + QB)
    ok0 = ok & ((k >= QB) | (p >= QB))
    mask_q = np.stack([ok0, ok], 1)
    kk, col = p, k
    okk = (kk >= col % QB) & (kk <= col % QB + QB)
    okk0 = okk & ((kk >= QB) | (col >= QB))
    mask_k = np.stack([okk0, okk], 1)
    NEG = -1e30
    sel = (p[:, :, None] % QUARTER == DG * np.arange(SUBS)[None, :, None] + k[:, None, :] // NS)
    sel_t = (np.arange(QUARTER)[None, None, :] == DG * np.arange(SUBS)[None, :, None] + p[:, :, None] // NS)
    return {
        "ident": np.eye(P, dtype=f), "ident16": np.eye(P, dtype=np.float16),
        "masks": np.stack([np.where(m, 0, NEG) for m in (mask_q, mask_k)], 1).astype(f),
        "cos": np.cos(ang).astype(f), "sin": np.sin(ang).astype(f), "nsin": (-np.sin(ang)).astype(f),
        "iota": np.tile(np.arange(E, dtype=f), (P, 1)),
        "sel": sel.reshape(P, SUBS * P).astype(np.float16), "selT": sel_t.reshape(P, SUBS * QUARTER).astype(f),
    }


PHASES = 4


def kernel(**inputs):
    import concourse.bacc as bacc
    from concourse.bass_utils import run_bass_kernel_spmd

    a = {n: np.asarray(v) for n, v in inputs.items()}
    lay = {
        "x": a["L0_attn_a_x"].reshape(BATCH * T, C),
        "qkvT": a["L0_attn_a_w_attn"].T, "projT": a["L0_attn_a_w_proj"].T,
        "g": a["L0_ffn_Wg"],
        "w1": a["L0_ffn_W1"].transpose(1, 0, 2), "w2": a["L0_ffn_W2"].transpose(1, 0, 2),
        "w3": a["L0_ffn_W3"].reshape(E, HC, P, C).transpose(2, 0, 1, 3),
        "A": a["L0_attn_b_A_log"].reshape(QUARTERS, SUBS, DG * NS).transpose(2, 1, 0).reshape(P, G),
        "D": a["L0_attn_b_D"].reshape(P, 1), "dtb": a["L0_attn_b_dt_proj_b"].reshape(P, 1),
        "xpT": a["L0_attn_b_x_proj_w"].T, "dtT": a["L0_attn_b_dt_proj_w"].T,
        "BT": np.tile(a["L0_attn_b_B_proj_w"].T, (1, DG)), "CT": np.tile(a["L0_attn_b_C_proj_w"].T, (1, DG)),
    }
    lay.update(constants())
    arrays = {n + "_dram": np.ascontiguousarray(v) for n, v in lay.items()}
    nc = bacc.Bacc("TRN2", target_bir_lowering=False, num_devices=1)
    dram = {n[:-5]: nc.dram_tensor(n, v.shape, mybir.dt.from_np(v.dtype), kind="ExternalInput").ap() for n, v in arrays.items()}
    out = nc.dram_tensor("out_dram", (BATCH * T, C), F32, kind="ExternalOutput").ap()
    build(nc, dram["x"], out, dram, PHASES)
    r = run_bass_kernel_spmd(nc, [arrays], core_ids=[0])
    return r.results[0]["out_dram"].reshape(BATCH, T, C)
```
